# Optimizing a Trainium2 kernel written in Bass

```python
import numpy as np
import jax
import jax.numpy as jnp

def _softmax(x, axis=-1):
    return jax.nn.softmax(x, axis=axis)

def _gelu(x):
    return jax.nn.gelu(x, approximate=True)

def _silu(x):
    return jax.nn.silu(x)

def _sigmoid(x):
    return jax.nn.sigmoid(x)

def _layernorm(x, axis=-1, eps=1e-05):
    m = jnp.mean(x, axis=axis, keepdims=True)
    v = jnp.var(x, axis=axis, keepdims=True)
    return (x - m) / jnp.sqrt(v + eps)

def _scatter_add(tgt, idx, src, axis=0):
    return tgt.at[idx].add(src)

def _segment_sum(src, seg, n):
    return jax.ops.segment_sum(src, seg, n)
kernel_name = 'mk_prb_d1_jaxref_r4_fd8524'

def setup_inputs(seed: int=0):
    np.random.seed(seed)
    _w = jnp.asarray

    def _L0_attn_setup():
        import jax, jax.numpy as jnp
        import numpy as np
        D_MODEL = 256
        NUM_HEADS = 16
        BATCH = 2
        SEQ = 512

        def _trunc_normal(key, shape, std):
            return jax.random.truncated_normal(key, -3.0, 3.0, shape, dtype=jnp.float32) * std
        key = jax.random.key(seed)
        kx, kq, kk, kv, ko = jax.random.split(key, 5)
        std = (2.0 / (D_MODEL + D_MODEL)) ** 0.5
        return {'X': jax.random.normal(kx, (BATCH, SEQ, D_MODEL), dtype=jnp.float32), 'q_proj': _trunc_normal(kq, (D_MODEL, D_MODEL), std), 'k_proj': _trunc_normal(kk, (D_MODEL, D_MODEL), std), 'v_proj': _trunc_normal(kv, (D_MODEL, D_MODEL), std), 'o_proj': _trunc_normal(ko, (D_MODEL, D_MODEL), std)}
    _L0_attn_in = _L0_attn_setup()

    def _L0_ffn_setup():
        import jax, jax.numpy as jnp
        import numpy as np
        DIM = 256

        def _reference_tuple_inner(x, W_r, W_k, W_v, mu_r, mu_k):
            B, T, C = x.shape
            x_prev = jnp.concatenate([jnp.zeros((B, 1, C), x.dtype), x[:, :-1, :]], axis=1)
            xr = mu_r * x + (1.0 - mu_r) * x_prev
            xk = mu_k * x + (1.0 - mu_k) * x_prev
            r = jax.nn.sigmoid(jnp.einsum('btc,dc->btd', xr, W_r))
            k = jnp.einsum('btc,dc->btd', xk, W_k)
            k_act = jnp.square(jax.nn.relu(k))
            out = r * jnp.einsum('btc,dc->btd', k_act, W_v)
            new_state = x[:, -1, :]
            return (out, new_state)
        key = jax.random.key(seed)
        ks = jax.random.split(key, 6)
        B, T, C = (8, 512, DIM)
        x = jax.random.normal(ks[0], (B, T, C), dtype=jnp.float32)
        s = 1.0 / np.sqrt(C)
        W_r = jax.random.uniform(ks[1], (C, C), jnp.float32, -s, s)
        W_k = jax.random.uniform(ks[2], (C, C), jnp.float32, -s, s)
        W_v = jax.random.uniform(ks[3], (C, C), jnp.float32, -s, s)
        mu_r = jax.random.uniform(ks[4], (C,), jnp.float32)
        mu_k = jax.random.uniform(ks[5], (C,), jnp.float32)
        return {'x': x, 'W_r': W_r, 'W_k': W_k, 'W_v': W_v, 'mu_r': mu_r, 'mu_k': mu_k}
    _L0_ffn_in = _L0_ffn_setup()
    _d = {'L0_attn_X': _L0_attn_in['X'], 'L0_attn_q_proj': _L0_attn_in['q_proj'], 'L0_attn_k_proj': _L0_attn_in['k_proj'], 'L0_attn_v_proj': _L0_attn_in['v_proj'], 'L0_attn_o_proj': _L0_attn_in['o_proj'], 'L0_ffn_W_r': _L0_ffn_in['W_r'], 'L0_ffn_W_k': _L0_ffn_in['W_k'], 'L0_ffn_W_v': _L0_ffn_in['W_v'], 'L0_ffn_mu_r': _L0_ffn_in['mu_r'], 'L0_ffn_mu_k': _L0_ffn_in['mu_k']}
    _x0 = _d['L0_attn_X']
    _d['L0_attn_X'] = jax.random.normal(jax.random.fold_in(jax.random.key(seed), 1), (32, 512, 256), dtype=_x0.dtype)
    del _x0
    return _d

def reference(L0_attn_X, L0_attn_q_proj, L0_attn_k_proj, L0_attn_v_proj, L0_attn_o_proj, L0_ffn_W_r, L0_ffn_W_k, L0_ffn_W_v, L0_ffn_mu_r, L0_ffn_mu_k):

    def _L0_attn_ref(X, q_proj, k_proj, v_proj, o_proj):
        import jax, jax.numpy as jnp
        import numpy as np
        D_MODEL = 256
        NUM_HEADS = 16
        BATCH = 2
        SEQ = 512

        def _trunc_normal(key, shape, std):
            return jax.random.truncated_normal(key, -3.0, 3.0, shape, dtype=jnp.float32) * std
        B, S, D = X.shape
        H = NUM_HEADS
        d_k = D // H
        q_w = q_proj.reshape(H, d_k, D)
        k_w = k_proj.reshape(H, d_k, D)
        v_w = v_proj.reshape(H, d_k, D)
        o_w = o_proj.reshape(D, H, d_k).transpose(1, 0, 2)
        q = jnp.einsum('hkd,bsd->bhsk', q_w, X)
        k = jnp.einsum('hkd,bsd->bhsk', k_w, X)
        v = jnp.einsum('hkd,bsd->bhsk', v_w, X)
        scale = 1.0 / jnp.sqrt(jnp.asarray(d_k, dtype=X.dtype))
        scores = jnp.einsum('bhqk,bhsk->bhqs', q, k) * scale
        causal = jnp.tril(jnp.ones((S, S), dtype=bool))
        scores = jnp.where(causal, scores, jnp.asarray(-jnp.inf, dtype=scores.dtype))
        attn = jax.nn.softmax(scores, axis=-1)
        attn_out = jnp.einsum('bhqs,bhsk->bhqk', attn, v)
        return jnp.einsum('hdv,bhsv->bsd', o_w, attn_out)

    def _L0_ffn_ref(x, W_r, W_k, W_v, mu_r, mu_k):
        import jax, jax.numpy as jnp
        import numpy as np
        DIM = 256

        def _reference_tuple_inner(x, W_r, W_k, W_v, mu_r, mu_k):
            B, T, C = x.shape
            x_prev = jnp.concatenate([jnp.zeros((B, 1, C), x.dtype), x[:, :-1, :]], axis=1)
            xr = mu_r * x + (1.0 - mu_r) * x_prev
            xk = mu_k * x + (1.0 - mu_k) * x_prev
            r = jax.nn.sigmoid(jnp.einsum('btc,dc->btd', xr, W_r))
            k = jnp.einsum('btc,dc->btd', xk, W_k)
            k_act = jnp.square(jax.nn.relu(k))
            out = r * jnp.einsum('btc,dc->btd', k_act, W_v)
            new_state = x[:, -1, :]
            return (out, new_state)
        return _reference_tuple_inner(x, W_r, W_k, W_v, mu_r, mu_k)[0]
    x = L0_attn_X
    xn = _layernorm(x, axis=-1)
    x = x + _L0_attn_ref(xn, L0_attn_q_proj, L0_attn_k_proj, L0_attn_v_proj, L0_attn_o_proj) + _L0_ffn_ref(xn, L0_ffn_W_r, L0_ffn_W_k, L0_ffn_W_v, L0_ffn_mu_r, L0_ffn_mu_k)
    return x

_drawn_inputs = setup_inputs


def setup_inputs(seed=0):
    import zlib

    import numpy as np

    out = dict(_drawn_inputs(seed))
    spreads = {}
    factors = {'L0_ffn_W_r': 3.214, 'L0_ffn_mu_r': 6.459}
    for name, (base, spread) in spreads.items():
        noise = np.random.default_rng([zlib.crc32(name.encode()), seed]).standard_normal(out[name].shape)
        drawn = base * np.exp(spread * noise) if base else spread * noise
        out[name] = jnp.asarray(drawn.astype(out[name].dtype))
    for name, factor in factors.items():
        out[name] = (out[name] * factor).astype(out[name].dtype)
    return out
```

```python
import concourse.bass as bass
from concourse import mybir
from contextlib import ExitStack


def attention_and_channel_mix(
    nc: bass.Bass,
    x: bass.AP,
    wq_t: bass.AP,
    wk_t: bass.AP,
    wv_t: bass.AP,
    wo_t: bass.AP,
    fr_t: bass.AP,
    fk_t: bass.AP,
    fv_t: bass.AP,
    mu: bass.AP,
    out: bass.AP,
):
    f32 = mybir.dt.float32
    f32r = mybir.dt.float32r
    bf16 = mybir.dt.bfloat16
    ALU = mybir.AluOpType
    ACT = mybir.ActivationFunctionType
    AX = mybir.AxisListType.X

    BATCH, SEQ, D = x.shape
    P = 128
    HEADS = 16
    DH = D // HEADS
    TILES = SEQ // P
    CH = D // P
    PAIRS = HEADS // 2
    GROUPS = 4
    HALF = P // 2
    SHIFT_ROW = 3 * DH
    VW = DH + 1
    SCALE = float(DH) ** -0.5
    EPS = 1e-5
    MASKED = -1.0e38

    UNITS = []
    for g in range(GROUPS):
        heads4 = [(pair, par) for pair in (2 * g, 2 * g + 1) for par in range(2)]
        UNITS += [(0, pair, par) for pair, par in heads4]
        UNITS += [(1, pair, par) for pair, par in heads4]
        UNITS += [(2, pair, None) for pair in (2 * g, 2 * g + 1)]
    NU = len(UNITS)
    GU = NU // GROUPS
    LOTS = [(g * GU + a, g * GU + z) for g in range(GROUPS) for a, z in ((0, 4), (4, 8), (8, 10))]
    NL = len(LOTS)
    LAG = 2
    NPB = 8
    NSB = 3
    lot_of = [n for n, (a, z) in enumerate(LOTS) for _ in range(a, z)]

    NR = 3
    A_SLOTS = NU + 1
    P_LIST = ["xT0", "xT1", "q0", "q1", "k0", "k1", "v0", "v1", "kf0", "kf1", "r0", "r1", "wv0", "wv1"]
    F_LIST = ["ot0", "ot1", "ot2", "ot3", "oc0", "oc1", "op0", "op1"]
    C_LIST = ["xT0", "xT1", "q0", "q1", "k0", "k1", "v0", "v1", "ot0", "ot1", "ot2", "ot3",
              "kf0", "kf1", "oc0", "oc1", "r0", "r1", "op0", "op1", "wv0", "wv1"]
    TURN = A_SLOTS + len(C_LIST)
    PRO = 2 * len(P_LIST) + A_SLOTS
    assert TURN % NR == 0 and PRO % NR == 0

    class Stage:

        def __init__(self, first, b, names):
            self.first, self.b, self.names = first, b, names

        def slot(self, name):
            g = self.first + (name if isinstance(name, int) else self.names.index(name))
            return g % NR, self.b * (TURN // NR) + g // NR

    def wait(eng, sem, value):
        if not (isinstance(value, int) and value <= 0):
            eng.wait_ge(sem, value)

    def alone(eng):
        eng.nop(nofuse=True)

    ctx = ExitStack()
    with ctx:
        def sb(name, shape, dt):
            return ctx.enter_context(nc.sbuf_tensor(name, shape, dt))

        def sem(name):
            return ctx.enter_context(nc.semaphore(name))

        q_stack = [sb(f"q_stack{p}", [P, 2, PAIRS, SEQ], f32r) for p in range(2)]
        k_stack = [sb(f"k_stack{p}", [P, PAIRS, SEQ], f32r) for p in range(2)]
        v_ones = [sb(f"v_ones{p}", [P, TILES, HEADS, VW], f32) for p in range(2)]
        probs = sb("probs", [P, NPB, SEQ], f32)
        relu_k = probs[:, 0:2, :]
        gate = probs[:, 2:4, :]
        o_cols = sb("o_cols", [P, GROUPS, SEQ], f32)
        split_a = sb("split_a", [P, 2, CH, SEQ], f32r)
        split_b = sb("split_b", [P, 2, CH, SEQ], f32r)
        xs = sb("xs", [P, 2, CH, SEQ + 2], f32r)
        x_in = sb("x_in", [P, TILES, D], f32)
        rows = sb("rows", [P, TILES, D], f32)
        acc = [sb(f"acc{p}", [P, TILES, D], f32) for p in range(2)]
        weight = {n: sb(f"w_{n}", [P, 2, CH, D], f32r)
                  for n in ("q", "k", "v", "o", "ra", "rb", "ka", "kb", "fv")}
        ident = sb("ident", [P, P], f32)
        ident_h = sb("ident_h", [P, P], bf16)
        mask_h = sb("mask_h", [P, P], bf16)
        maxes = sb("maxes", [P, 2, PAIRS, TILES], f32)
        shifts = sb("shifts", [2 * PAIRS * TILES, P], f32)
        zeros = sb("zeros", [PAIRS * TILES, P], f32)
        ones = sb("ones", [PAIRS * TILES, P], f32)
        mus = sb("mus", [P, 2, CH], f32)
        one_minus_mus = sb("one_minus_mus", [P, 2, CH], f32)
        stats = sb("stats", [P, TILES, 6], f32)
        mean_var = sb("mean_var", [P, TILES, 2], f32)
        neg_mean = sb("neg_mean", [P, TILES], f32)
        var_eps = sb("var_eps", [P, TILES], f32)
        rstd = sb("rstd", [P, TILES], f32)
        minus_half = sb("minus_half", [P, TILES], f32)
        inv_den = sb("inv_den", [P, TILES, HEADS], f32)

        bank = [ctx.enter_context(nc.psum_tensor(f"bank{n}", [P, SEQ], f32)) for n in range(NR)]
        score = [ctx.enter_context(nc.psum_tensor(f"score{n}", [P, SEQ], f32)) for n in range(NSB)]
        attn = [ctx.enter_context(nc.psum_tensor(f"attn{n}", [P, SEQ], f32)) for n in range(2)]

        weights_in, mus_in, ones_in = sem("weights_in"), sem("mus_in"), sem("ones_in")
        cleared, consts_ready, setup_step = sem("cleared"), sem("consts_ready"), sem("setup_step")
        x_loaded, x_used = sem("x_loaded"), sem("x_used")
        bn_ready, moments_ready, ln_scalars, rstd_ready, rows_ready = (
            sem("bn_ready"), sem("moments_ready"), sem("ln_scalars"), sem("rstd_ready"), sem("rows_ready"))
        filled = [sem(f"filled{n}") for n in range(NR)]
        drained = [sem(f"drained{n}") for n in range(NR)]
        x_hi, qk_hi, o_hi = sem("x_hi"), sem("qk_hi"), sem("o_hi")
        relu_ready, act_hi, squared, act_split = sem("relu_ready"), sem("act_hi"), sem("squared"), sem("act_split")
        inv_ready = sem("inv_ready")
        q_stacked, k_stacked, shift_in, stored = sem("q_stacked"), sem("k_stacked"), sem("shift_in"), sem("stored")
        score_filled, exp_done, masked, lot_done, o_copied = (
            sem("score_filled"), sem("exp_done"), sem("masked"), sem("lot_done"), sem("o_copied"))

        QD, KD = 16 * (2 * CH * 0 + 6 + 2), 16 * 6

        def schedule(do_ab, do_c):
            do_c(Stage(0, 0, P_LIST), None, 0, 0)
            do_ab(Stage(len(P_LIST), 0, None), None, 0, 1)
            do_c(Stage(len(P_LIST) + A_SLOTS, 0, P_LIST), None, 1, 1)

            def turn(b, parity):
                do_ab(Stage(PRO, b, None), b, b + 1, parity)
                do_c(Stage(PRO + A_SLOTS, b, C_LIST), b, b + 2, parity)

            turn(0, 0)
            turn(1, 1)
            return turn

        def epilogue(do_ab, do_c):
            last = BATCH - 2
            end = PRO + TURN * last
            do_ab(Stage(end, 0, None), last, last + 1, 0)
            do_c(Stage(end + A_SLOTS, 0, F_LIST), last, None, 0)
            do_ab(None, last + 1, None, 1)
            do_c(Stage(end + A_SLOTS + len(F_LIST), 0, F_LIST), last + 1, None, 1)

        def run(eng, do_ab, do_c):
            turn = schedule(do_ab, do_c)
            with eng.Fori(1, (BATCH - 2) // 2) as i:
                turn(i * 2, 0)
                turn(i * 2 + 1, 1)
            epilogue(do_ab, do_c)

        block = ctx.enter_context(nc.Block())

        @block.sync
        def _(sp):
            for n, w in enumerate((wq_t, wk_t, wv_t, wo_t, fr_t, fk_t, fv_t)):
                sp.dma_start(probs[:, n, :], w).then_inc(weights_in, 16)
            sp.dma_start(mus[:, :, :], mu).then_inc(mus_in, 16)

            def load_x(b):
                sp.dma_start(x_in[:, :, :], x[bass.ds(b, 1), :, :].rearrange("b (t p) d -> p (b t) d", p=P)
                             ).then_inc(x_loaded, 16)

            load_x(0)
            sp.wait_ge(cleared, 3)
            for p in range(2):
                for par in range(2):
                    r = HALF * par + SHIFT_ROW
                    sp.dma_start(k_stack[p][r:r + 1, :, :].bitcast(f32), ones[:, :]).then_inc(ones_in, 16)

            def do_ab(st, b, c, parity):
                if c is None:
                    return
                bank_n, uses = st.slot(NU)
                sp.wait_ge(drained[bank_n], uses + 1)
                for par in range(2):
                    r, rows_n = HALF * par + SHIFT_ROW, PAIRS * TILES
                    sp.dma_start(q_stack[1 - parity][r:r + 1, par, :, :].bitcast(f32),
                                 shifts[par * rows_n:(par + 1) * rows_n, :]).then_inc(shift_in, 16)

            def do_c(st, b, c, parity):
                if c is not None:
                    qs, ks = q_stack[parity], k_stack[parity]
                    if b is not None:
                        sp.wait_ge(score_filled, NU * (b + 1))
                        alone(sp)
                        sp.wait_ge(shift_in, 32 * (b + 1))
                    for par in range(2):
                        r = HALF * par + SHIFT_ROW
                        sp.dma_start(qs[r:r + 1, par, :, :].bitcast(f32), zeros[:, :]).then_inc(q_stacked, 16)
                    for names, src, terms, done in ((("q0", "q1"), split_a, (0, 0, 1), q_stacked),
                                                    (("k0", "k1"), split_b, (0, 1, 0), k_stacked)):
                        for name in names:
                            bank_n, uses = st.slot(name)
                            sp.wait_ge(drained[bank_n], uses + 1)
                        for par in range(2):
                            for n, part in enumerate(terms):
                                r = HALF * par + DH * n
                                dst = (qs[r:r + DH, par, :, :] if src is split_a else ks[r:r + DH, :, :])
                                sp.dma_start(dst.bitcast(f32),
                                             src[HALF * par:HALF * (par + 1), part, :, :].bitcast(f32)
                                             ).then_inc(done, 16)
                if b is not None:
                    bank_n, uses = st.slot("op1")
                    sp.wait_ge(drained[bank_n], uses + 1)
                    sp.dma_start(out[bass.ds(b, 1), :, :].rearrange("b (t p) d -> p (b t) d", p=P),
                                 acc[parity][:, :, :]).then_inc(stored, 16)
                if c is not None and not (isinstance(c, int) and c == BATCH - 1):
                    sp.wait_ge(x_used, 2 * (c + 1))
                    load_x(c + 1)

            def turn_end(turn):
                turn(BATCH - 4, 0)
                turn(BATCH - 3, 1)

            turn = schedule(do_ab, do_c)
            with sp.Fori(1, (BATCH - 2) // 2 - 1) as i:
                turn(i * 2, 0)
                turn(i * 2 + 1, 1)
            turn_end(turn)
            epilogue(do_ab, do_c)
            sp.wait_ge(stored, 16 * BATCH)

        @block.gpsimd
        def _(pool):
            nc.gpsimd.memset(zeros[:, :], 0.0).then_inc(cleared, 1)
            nc.gpsimd.memset(ones[:, :], 1.0).then_inc(cleared, 1)
            nc.gpsimd.memset(minus_half[:, :], -0.5).then_inc(consts_ready, 1)
            nc.gpsimd.memset(ident[:, :], 1.0).then_inc(consts_ready, 1)
            nc.gpsimd.memset(ident_h[:, :], 1.0).then_inc(consts_ready, 1)
            nc.gpsimd.memset(mask_h[:, :], 0.0).then_inc(consts_ready, 1)
            pool.wait_ge(consts_ready, 4)
            for m in (ident, ident_h):
                nc.gpsimd.affine_select(out=m[:, :], in_=m[:, :], compare_op=ALU.is_equal, fill=0.0, base=0,
                                        pattern=[[-1, P]], channel_multiplier=1).then_inc(consts_ready, 1)
            nc.gpsimd.affine_select(out=mask_h[:, :], in_=mask_h[:, :], compare_op=ALU.is_ge, fill=MASKED, base=0,
                                    pattern=[[-1, P]], channel_multiplier=1).then_inc(consts_ready, 1)

            def layernorm(c, last_read):
                wait(pool, ln_scalars, 2 * (c + 1))
                nc.gpsimd.tensor_tensor(rstd[:, :], var_eps[:, :], minus_half[:, :], ALU.pow).then_inc(rstd_ready, 1)
                wait(pool, rstd_ready, c + 1)
                if last_read is not None:
                    pool.wait_ge(filled[last_read[0]], last_read[1] + 1)
                alone(pool)
                for t in range(TILES):
                    nc.gpsimd.tensor_scalar(rows[:, t, :], x_in[:, t, :], neg_mean[:, t:t + 1], rstd[:, t:t + 1],
                                            ALU.add, ALU.mult).then_inc(rows_ready, 1)

            def do_ab(st, b, c, parity):
                for n, (kind, _, _) in enumerate(UNITS):
                    if b is not None:
                        pool.wait_ge(exp_done, NU * b + n + 1)
                        alone(pool)
                        tile = probs[:, n % NPB, :]
                        if kind == 0:
                            view, pattern = tile[:, 0:P], [[1, P]]
                        else:
                            apart = SEQ - P if kind == 1 else SEQ // 2
                            view = tile.rearrange("p (a k) -> p a k", k=P)[:, 0::apart // P, :]
                            pattern = [[0, 2], [1, P]]
                        nc.gpsimd.affine_select(out=view, in_=view, compare_op=ALU.is_ge, fill=0.0, base=0,
                                                pattern=pattern, channel_multiplier=-1).then_inc(masked, 1)
                    if n == NU // 2 and b is not None and c is not None and not (isinstance(c, int) and c == BATCH - 1):
                        if isinstance(b, int) and b == 0:
                            last = Stage(len(P_LIST) + A_SLOTS, 0, P_LIST).slot("xT1")
                        else:
                            last = Stage(PRO + A_SLOTS - TURN, b, C_LIST).slot("oc1")
                        layernorm(c + 1, last)
                if b is None:
                    layernorm(1, Stage(0, 0, P_LIST).slot("xT1"))

            def do_c(st, b, c, parity):
                if c is None:
                    return
                for m in range(CH):
                    wait(pool, act_hi, CH * c + m + 1)
                    nc.gpsimd.tensor_tensor(relu_k[:, m, :], relu_k[:, m, :], relu_k[:, m, :], ALU.mult
                                            ).then_inc(squared, 1)
                for m in range(2):
                    bank_n, uses = st.slot(f"wv{m}")
                    pool.wait_ge(drained[bank_n], uses + 1)
                    if b is not None:
                        pool.wait_ge(stored, 16 * (b + 1))
                    nc.gpsimd.tensor_tensor(
                        acc[parity][:, 2 * m:2 * m + 2, :], gate[:, m, :].rearrange("p (t d) -> p t d", t=2),
                        x_in[:, 2 * m:2 * m + 2, :], ALU.add).then_inc(x_used, 1)

            layernorm(0, None)
            run(pool, do_ab, do_c)

        @block.scalar
        def _(act):
            def do_ab(st, b, c, parity):
                for n, (kind, pair, par) in enumerate(UNITS):
                    if b is None:
                        continue
                    act.wait_ge(score_filled, NU * b + n + 1)
                    wait(act, lot_done, NL * b + (lot_of[n - NPB] + 1 if n >= NPB else lot_of[NU + n - NPB] + 1 - NL))
                    if n in (0, 2) and not (isinstance(b, int) and b == BATCH - 1):
                        act.wait_ge(act_split if n == 0 else x_used, 2 * (b + 2))
                    nc.scalar.activation(probs[:, n % NPB, :], score[n % NSB][:, :], ACT.Exp).then_inc(exp_done, 1)
                    if n >= GU and n % GU == 5:
                        copy_out(b, n // GU - 1)
                if b is not None:
                    copy_out(b, GROUPS - 1)
                if c is not None:
                    bank_n, uses = st.slot(NU)
                    act.wait_ge(filled[bank_n], uses + 1)
                    wait(act, shift_in, 32 * c)
                    nc.scalar.mul(shifts[:, :], bank[bank_n][0:2 * PAIRS * TILES, 0:P], -1.0
                                  ).then_inc(drained[bank_n], 1)

            def copy_out(b, g):
                act.wait_ge(lot_done, NL * b + 3 * (g + 1))
                nc.scalar.copy(o_cols[:, g, :], attn[g % 2][:, :]).then_inc(o_copied, 1)

            def do_c(st, b, c, parity):
                for name in st.names:
                    kind, m = name[:-1], int(name[-1])
                    if kind in ("ot", "op", "wv"):
                        continue
                    bank_n, uses = st.slot(name)
                    act.wait_ge(filled[bank_n], uses + 1)
                    src = bank[bank_n][:, :]
                    if kind == "xT":
                        nc.scalar.copy(xs[:, 0, m, 2:SEQ + 2], src).then_inc(x_hi, 1)
                    if kind == "q":
                        nc.scalar.mul(split_a[:, 0, m, :], src, SCALE).then_inc(qk_hi, 1)
                    if kind == "k":
                        nc.scalar.copy(split_b[:, 0, m, :], src).then_inc(qk_hi, 1)
                    if kind == "v":
                        nc.scalar.copy(v_ones[parity][:, 2 * m:2 * m + 2, :, 0:DH],
                                       src.rearrange("p (t h d) -> p t h d", t=2, h=HEADS)
                                       ).then_inc(drained[bank_n], 1)
                    if kind == "kf":
                        nc.scalar.activation(relu_k[:, m, :], src, ACT.Relu).then_inc(drained[bank_n], 1)
                        act.wait_ge(drained[bank_n], uses + 1)
                        wait(act, k_stacked, KD * (c + 1))
                        nc.scalar.activation(split_b[:, 0, m, :], relu_k[:, m, :], ACT.Square).then_inc(act_hi, 1)
                    if kind == "oc":
                        if c is not None:
                            wait(act, q_stacked, QD * (c + 1))
                        nc.scalar.copy(split_a[:, 0, m, :], src).then_inc(o_hi, 1)
                    if kind == "r":
                        nc.scalar.activation(gate[:, m, :], src, ACT.Tanh, scale=0.5).then_inc(drained[bank_n], 1)

            run(act, do_ab, do_c)

        @block.vector
        def _(dve):
            steps = [0]

            def step(ins):
                steps[0] += 1
                ins.then_inc(setup_step, 1)
                dve.wait_ge(setup_step, steps[0])

            for p in range(2):
                step(nc.vector.memset(q_stack[p][:, :, :, :].bitcast(f32), 0.0))
                step(nc.vector.memset(k_stack[p][:, :, :].bitcast(f32), 0.0))
                step(nc.vector.memset(v_ones[p][:, :, :, :], 1.0))
                step(nc.vector.memset(attn[p][:, :], 0.0))
            nc.vector.memset(xs[:, :, :, 0:2].bitcast(f32), 0.0).then_inc(cleared, 1)

            dve.wait_ge(weights_in, 16 * 7)
            dve.wait_ge(mus_in, 16)
            step(nc.vector.tensor_scalar(one_minus_mus[:, :, :], mus[:, :, :], -1.0, 1.0, ALU.mult, ALU.add))
            step(nc.vector.tensor_scalar(probs[:, 6, :], probs[:, 6, :], 0.5, None, ALU.mult))

            def split(name, src):
                hi, lo = (weight[name][:, n, :, :] for n in range(2))
                src = src.rearrange("p (c d) -> p c d", c=CH)
                step(nc.vector.tensor_copy(hi, src))
                step(nc.vector.tensor_tensor(lo, src, hi.bitcast(f32), ALU.subtract))

            for n, name in enumerate(("q", "k", "v", "o")):
                split(name, probs[:, n, :])
            split("fv", probs[:, 6, :])
            for n, name in enumerate("rk"):
                for half, factor in (("a", mus), ("b", one_minus_mus)):
                    for c in range(CH):
                        step(nc.vector.tensor_scalar(probs[:, 7, c * D:(c + 1) * D], probs[:, 4 + n, c * D:(c + 1) * D],
                                                     factor[:, n, c:c + 1], None, ALU.mult))
                    split(name + half, probs[:, 7, :])

            def layernorm(c):
                dve.wait_ge(x_loaded, 16 * (c + 1))
                for t in range(TILES):
                    nc.vector.bn_stats(stats[:, t, :], x_in[:, t, :]).then_inc(bn_ready, 1)
                dve.wait_ge(bn_ready, TILES * (c + 1))
                alone(dve)
                for t in range(TILES):
                    nc.vector.bn_aggr(mean_var[:, t, :], stats[:, t, :]).then_inc(moments_ready, 1)
                dve.wait_ge(moments_ready, TILES * (c + 1))
                wait(dve, rows_ready, TILES * c)
                nc.vector.tensor_scalar(neg_mean[:, :], mean_var[:, :, 0], -1.0, None, ALU.mult).then_inc(ln_scalars, 1)
                nc.vector.tensor_scalar(var_eps[:, :], mean_var[:, :, 1], EPS, None, ALU.add).then_inc(ln_scalars, 1)

            def do_ab(st, b, c, parity):
                if c is not None:
                    for n, (kind, pair, par) in enumerate(UNITS):
                        bank_n, uses = st.slot(n)
                        dve.wait_ge(filled[bank_n], uses + 1)
                        src = bank[bank_n]
                        if kind == 0:
                            ins = nc.vector.tensor_reduce(maxes[:, par, pair, 3:4], src[:, :], AX, ALU.max)
                        if kind == 1:
                            nc.vector.tensor_reduce(maxes[:, par, pair, 2:3], src[:, 0:SEQ - P], AX, ALU.max)
                            ins = nc.vector.tensor_reduce(maxes[:, par, pair, 0:1], src[:, SEQ - P:SEQ], AX, ALU.max)
                        if kind == 2:
                            ins = nc.vector.tensor_reduce(maxes[:, :, pair, 1], src[:, :].rearrange("p (a k) -> p a k", a=2),
                                                          AX, ALU.max)
                        ins.then_inc(drained[bank_n], 1)
                        if n == NU // 4 and b is not None and not (isinstance(c, int) and c == BATCH - 1):
                            layernorm(c + 1)
                if b is None:
                    layernorm(1)

            def do_c(st, b, c, parity):
                for name in st.names:
                    kind, m = name[:-1], int(name[-1])
                    bank_n, uses = st.slot(name)
                    src = bank[bank_n][:, :]
                    if kind == "xT":
                        dve.wait_ge(x_hi, CH * c + m + 1)
                        nc.vector.tensor_tensor(xs[:, 1, m, 2:SEQ + 2], src, xs[:, 0, m, 2:SEQ + 2].bitcast(f32),
                                                ALU.subtract).then_inc(drained[bank_n], 1)
                    if kind == "q":
                        dve.wait_ge(qk_hi, 2 * CH * c + m + 1)
                        nc.vector.scalar_tensor_tensor(split_a[:, 1, m, :], src, SCALE, split_a[:, 0, m, :].bitcast(f32),
                                                       ALU.mult, ALU.subtract).then_inc(drained[bank_n], 1)
                    if kind == "k":
                        dve.wait_ge(qk_hi, 2 * CH * c + CH + m + 1)
                        nc.vector.tensor_tensor(split_b[:, 1, m, :], src, split_b[:, 0, m, :].bitcast(f32),
                                                ALU.subtract).then_inc(drained[bank_n], 1)
                    if kind == "ot":
                        dve.wait_ge(filled[bank_n], uses + 1)
                        per_head = src.rearrange("p (h d) -> p h d", h=HEADS)
                        nc.vector.reciprocal(inv_den[:, m, :], per_head[:, :, DH]).then_inc(inv_ready, 1)
                        dve.wait_ge(inv_ready, TILES * b + m + 1)
                        nc.vector.tensor_tensor(rows[:, m, :].rearrange("p (h d) -> p h d", h=HEADS), per_head[:, :, 0:DH],
                                                inv_den[:, m, :].unsqueeze(2).to_broadcast([P, HEADS, DH]), ALU.mult
                                                ).then_inc(drained[bank_n], 1)
                    if kind == "kf":
                        dve.wait_ge(squared, CH * c + m + 1)
                        nc.vector.tensor_tensor(split_b[:, 1, m, :], relu_k[:, m, :], split_b[:, 0, m, :].bitcast(f32),
                                                ALU.subtract).then_inc(act_split, 1)
                    if kind == "oc":
                        dve.wait_ge(o_hi, CH * b + m + 1)
                        nc.vector.tensor_tensor(split_a[:, 1, m, :], src, split_a[:, 0, m, :].bitcast(f32),
                                                ALU.subtract).then_inc(drained[bank_n], 1)
                    if kind == "op":
                        dve.wait_ge(filled[bank_n], uses + 1)
                        dve.wait_ge(x_used, 2 * (b + 1))
                        nc.vector.tensor_tensor(acc[parity][:, 2 * m:2 * m + 2, :], src.rearrange("p (t d) -> p t d", t=2),
                                                acc[parity][:, 2 * m:2 * m + 2, :], ALU.add).then_inc(drained[bank_n], 1)
                    if kind == "wv":
                        dve.wait_ge(filled[bank_n], uses + 1)
                        r_bank, r_uses = st.slot(f"r{m}")
                        dve.wait_ge(drained[r_bank], r_uses + 1)
                        nc.vector.scalar_tensor_tensor(gate[:, m, :], gate[:, m, :], 1.0, src, ALU.add, ALU.mult
                                                       ).then_inc(drained[bank_n], 1)

            layernorm(0)
            run(dve, do_ab, do_c)

        @block.tensor
        def _(pe):
            pe.wait_ge(consts_ready, 7)
            pe.wait_ge(cleared, 3)
            pe.wait_ge(ones_in, 16 * 4)
            pe.wait_ge(setup_step, 1)

            def open_slot(st, name):
                bank_n, uses = st.slot(name)
                if name == "kf0" or not (isinstance(uses, int) and uses == 0):
                    wait(pe, drained[bank_n], uses)
                return bank_n, bank[bank_n]

            def maxima(st, c, n, parity):
                kind, pair, par = UNITS[n]
                qs, ks = q_stack[parity], k_stack[parity]
                bank_n, dst = open_slot(st, n)
                if kind == 0:
                    parts = [(0, SEQ, par, 3)]
                    masks = dst[:, SEQ - P:SEQ], mask_h[:, :]
                if kind == 1:
                    parts = [(0, SEQ - P, par, 2), (SEQ - P, P, par, 0)]
                    masks = dst[:, SEQ // 2:SEQ], mask_h[:, :].unsqueeze(1).to_broadcast([P, 2, P])
                if kind == 2:
                    parts = [(0, SEQ // 2, 0, 1), (SEQ // 2, SEQ // 2, 1, 1)]
                    masks = (dst[:, :].rearrange("p (a k) -> p a k", k=P)[:, 1::2, :],
                             mask_h[:, :].unsqueeze(1).to_broadcast([P, 2, P]))
                for i, (at, keys, pr, tile) in enumerate(parts):
                    nc.tensor.matmul(dst[:, at:at + keys], qs[:, pr, pair, tile * P:(tile + 1) * P], ks[:, pair, 0:keys],
                                     start=(i == 0), stop=False, skip_group_check=True)
                nc.tensor.matmul(masks[0], ident_h[:, :], masks[1], start=False, stop=True, skip_group_check=True
                                 ).then_inc(filled[bank_n], 1)

            def scores(b, n, parity):
                kind, pair, par = UNITS[n]
                qs, ks = q_stack[parity], k_stack[parity]
                dst = score[n % NSB]
                before = n - NSB if n >= NSB else NU - 1 - (NU - 1 - n) % NSB - NU
                wait(pe, exp_done, NU * b + before + 1)
                if kind == 0:
                    parts = [(0, par, 0)]
                if kind == 1:
                    parts = [(0, par, 1), (SEQ - P, par, 3)]
                if kind == 2:
                    parts = [(0, 0, 2), (SEQ // 2, 1, 2)]
                for at, pr, tile in parts:
                    queries = SEQ - tile * P
                    ins = nc.tensor.matmul(dst[:, at:at + queries], ks[:, pair, tile * P:(tile + 1) * P],
                                           qs[:, pr, pair, tile * P:SEQ], start=True, stop=True)
                ins.then_inc(score_filled, 1)

            def lot(b, n, parity):
                first, end = LOTS[n]
                g = n // 3
                if n % 3 == 0:
                    wait(pe, o_copied, GROUPS * b + g - 1)
                pe.wait_ge(masked, NU * b + end)
                todo = []
                for u in range(first, end):
                    kind, pair, par = UNITS[u]
                    if kind == 0:
                        todo += [(0, u, pair, par, 0, 0)]
                    if kind == 1:
                        todo += [(0, u, pair, par, 0, 1), (1, u, pair, par, SEQ - P, 3)]
                    if kind == 2:
                        todo += [(0, u, pair, 0, 0, 2), (0, u, pair, 1, SEQ // 2, 2)]
                todo.sort(key=lambda x: x[0])
                for _, u, pair, par, at, tile in todo:
                    quad = (pair % 2) * 2 + par
                    head = 4 * g + quad
                    queries = SEQ - tile * P
                    ins = nc.tensor.matmul(attn[g % 2][32 * quad:32 * quad + VW, tile * P:SEQ],
                                           v_ones[parity][:, tile, head, :], probs[:, u % NPB, at:at + queries],
                                           start=(tile == 0), stop=(tile == 2), skip_group_check=True)
                ins.then_inc(lot_done, 1)

            def do_ab(st, b, c, parity):
                if c is not None:
                    pe.wait_ge(q_stacked, QD * (c + 1))
                    pe.wait_ge(k_stacked, KD * (c + 1))
                if b is not None:
                    pe.wait_ge(shift_in, 32 * (b + 1))
                todo = list(range(NL))
                for n in range(NU):
                    if c is not None:
                        maxima(st, c, n, 1 - parity)
                    if b is not None:
                        scores(b, n, parity)
                        if todo and LOTS[todo[0]][1] - 1 + LAG <= n:
                            lot(b, todo.pop(0), parity)
                if c is not None:
                    bank_n, dst = open_slot(st, NU)
                    last, uses = st.slot(NU - 1)
                    pe.wait_ge(drained[last], uses + 1)
                    alone(pe)
                    nc.tensor.transpose(dst[0:2 * PAIRS * TILES, 0:P], maxes[:, :, :, :].rearrange("p a b c -> p (a b c)"),
                                        ident[:, :]).then_inc(filled[bank_n], 1)
                if b is not None:
                    for n in todo:
                        lot(b, n, parity)

            def products(dst, pairs):
                for n, (lhs, rhs) in enumerate(pairs):
                    ins = nc.tensor.matmul(dst, lhs, rhs, start=(n == 0), stop=(n == len(pairs) - 1))
                return ins

            SPLIT = ((0, 0), (0, 1), (1, 0))

            def columns(dst, m, sources):
                return products(dst[:, :], [(w[:, pw, c, m * P:(m + 1) * P], a(pa, c))
                                            for pa, pw in SPLIT for a, w in sources for c in range(CH)])

            def tokens(dst, m, sources):
                for i in range(2):
                    cut = slice((2 * m + i) * P, (2 * m + i + 1) * P)
                    ins = products(dst[:, i * D:(i + 1) * D], [(a(pa, c)[:, cut], w[:, pw, c, :])
                                                              for pa, pw in SPLIT for a, w in sources for c in range(CH)])
                return ins

            def now(part, c):
                return xs[:, part, c, 2:SEQ + 2]

            def before(part, c):
                return xs[:, part, c, 1:SEQ + 1]

            def part_a(part, c):
                return split_a[:, part, c, :]

            def part_b(part, c):
                return split_b[:, part, c, :]

            def do_c(st, b, c, parity):
                for name in st.names:
                    kind, m = name[:-1], int(name[-1])
                    bank_n, dst = open_slot(st, name)
                    if kind == "xT":
                        wait(pe, rows_ready, TILES * (c + 1))
                        for t in range(TILES):
                            ins = nc.tensor.transpose(dst[:, t * P:(t + 1) * P], rows[:, t, m * P:(m + 1) * P], ident[:, :])
                    if kind in ("q", "k"):
                        if name == "q0":
                            for x_name in ("xT0", "xT1"):
                                x_bank, uses = st.slot(x_name)
                                pe.wait_ge(drained[x_bank], uses + 1)
                        ins = columns(dst, m, [(now, weight[kind])])
                    if kind == "v":
                        ins = tokens(dst, m, [(now, weight["v"])])
                    if kind == "kf":
                        ins = columns(dst, m, [(now, weight["ka"]), (before, weight["kb"])])
                    if kind == "r":
                        ins = tokens(dst, m, [(now, weight["ra"]), (before, weight["rb"])])
                    if kind == "ot":
                        wait(pe, o_copied, GROUPS * (b + 1))
                        for g in range(GROUPS):
                            ins = nc.tensor.transpose(dst[:, g * P:(g + 1) * P], o_cols[:, g, m * P:(m + 1) * P], ident[:, :])
                    if kind == "oc":
                        for t in range(TILES):
                            if m == 0:
                                t_bank, uses = st.slot(f"ot{t}")
                                pe.wait_ge(drained[t_bank], uses + 1)
                            ins = nc.tensor.transpose(dst[:, t * P:(t + 1) * P], rows[:, t, m * P:(m + 1) * P], ident[:, :])
                    if kind == "op":
                        if m == 0:
                            for o_name in ("oc0", "oc1"):
                                o_bank, uses = st.slot(o_name)
                                pe.wait_ge(drained[o_bank], uses + 1)
                        ins = tokens(dst, m, [(part_a, weight["o"])])
                    if kind == "wv":
                        pe.wait_ge(act_split, CH * (c + 1))
                        ins = tokens(dst, m, [(part_b, weight["fv"])])
                    ins.then_inc(filled[bank_n], 1)

            run(pe, do_ab, do_c)


def kernel(L0_attn_X, L0_attn_q_proj, L0_attn_k_proj, L0_attn_v_proj, L0_attn_o_proj,
           L0_ffn_W_r, L0_ffn_W_k, L0_ffn_W_v, L0_ffn_mu_r, L0_ffn_mu_k):
    import numpy as np
    import concourse.bacc as bacc
    from concourse.bass_utils import run_bass_kernel_spmd

    D, DH, P = 256, 16, 128

    def chunks(w):
        return np.ascontiguousarray(w.reshape(D // P, P, D).transpose(1, 0, 2).reshape(P, -1))

    def arr(a):
        return np.asarray(a)

    def for_stack(w):
        return arr(w).reshape(2, 4, 2, DH, D).transpose(4, 0, 2, 3, 1).reshape(D, D)

    data = {
        "x": arr(L0_attn_X),
        "wq_t": chunks(for_stack(L0_attn_q_proj)),
        "wk_t": chunks(for_stack(L0_attn_k_proj)),
        "wv_t": chunks(arr(L0_attn_v_proj).reshape(2, 4, 2, DH, D).transpose(4, 1, 0, 2, 3).reshape(D, D)),
        "wo_t": chunks(arr(L0_attn_o_proj).reshape(D, 2, 4, 2, DH).transpose(2, 1, 3, 4, 0).reshape(D, D)),
        "fr_t": chunks(arr(L0_ffn_W_r).T),
        "fk_t": chunks(arr(L0_ffn_W_k).T),
        "fv_t": chunks(arr(L0_ffn_W_v).T),
        "mu": np.ascontiguousarray(np.stack([arr(L0_ffn_mu_r), arr(L0_ffn_mu_k)]).reshape(2, D // P, P).transpose(2, 0, 1)),
    }
    nc = bacc.Bacc("TRN2", target_bir_lowering=False, num_devices=1)
    args = {n: nc.dram_tensor(n, a.shape, mybir.dt.from_np(a.dtype), kind="ExternalInput").ap() for n, a in data.items()}
    out = nc.dram_tensor("out", data["x"].shape, mybir.dt.float32, kind="ExternalOutput").ap()
    attention_and_channel_mix(nc, **args, out=out)
    got = run_bass_kernel_spmd(nc, [data], core_ids=[0])
    return got.results[0]["out"]
```

```python
import concourse.bass as bass
from concourse import mybir
from contextlib import ExitStack


def attention_and_channel_mix(
    nc: bass.Bass,
    x: bass.AP,
    wq_t: bass.AP,
    wk_t: bass.AP,
    wv_t: bass.AP,
    wo_t: bass.AP,
    fr_t: bass.AP,
    fk_t: bass.AP,
    fv_t: bass.AP,
    mu: bass.AP,
    out: bass.AP,
):
    f32 = mybir.dt.float32
    f32r = mybir.dt.float32r
    bf16 = mybir.dt.bfloat16
    ALU = mybir.AluOpType
    ACT = mybir.ActivationFunctionType
    AX = mybir.AxisListType.X

    BATCH, SEQ, D = x.shape
    P = 128
    HEADS = 16
    DH = D // HEADS
    TILES = SEQ // P
    CH = D // P
    PAIRS = HEADS // 2
    GROUPS = 4
    HALF = P // 2
    SHIFT_ROW = 3 * DH
    VW = DH + 1
    SCALE = float(DH) ** -0.5
    EPS = 1e-5
    MASKED = -1.0e38
    LOWEST = -3.4e38

    UNITS = []
    for g in range(GROUPS):
        heads4 = [(pair, par) for pair in (2 * g, 2 * g + 1) for par in range(2)]
        UNITS += [(0, pair, par) for pair, par in heads4]
        UNITS += [(1, pair, par) for pair, par in heads4]
        UNITS += [(2, pair, None) for pair in (2 * g, 2 * g + 1)]
    NU = len(UNITS)
    GU = NU // GROUPS
    def max_parts(kind, par):
        return {0: [(0, par, 3)], 1: [(0, par, 2), (SEQ - P, par, 0)], 2: [(0, 0, 1), (SEQ // 2, 1, 1)]}[kind]

    LOTS = [(g * GU + a, g * GU + z) for g in range(GROUPS) for a, z in ((0, 4), (4, 8), (8, 10))]
    NL = len(LOTS)
    LAG = 3
    NPB = 8
    RESIDUAL_UNITS = [4, 6]
    LN_UNITS = [13, 15, 18, 20, 22]
    ROWS_UNITS = [24, 26, 28, 29, 31]
    SPLIT_UNITS = [35, 37]
    NSB = 3
    lot_of = [n for n, (a, z) in enumerate(LOTS) for _ in range(a, z)]

    NR = 3
    MIXES = 2 * CH
    XT_AT = NU - 6
    A_LIST = [*range(XT_AT), "xT0", "xT1", *range(XT_AT, NU), "turned"]
    X_LIST = ["xT0", "xT1"]
    P_LIST = ["q0", "q1", "k0", "k1", "v0", "v1", "kf0", "kf1", "r0", "r1", "wv0", "wv1"]
    F_LIST = ["ot0", "ot1", "ot2", "ot3", "oc0", "oc1", "op0", "op1"]
    C_LIST = ["q0", "q1", "k0", "k1", "v0", "ot0", "v1", "ot1", "kf0", "ot2", "kf1", "ot3",
              "r0", "oc0", "oc1", "r1", "op0", "wv0", "op1", "wv1"]
    TURN = len(A_LIST) + len(C_LIST)
    PRO = len(X_LIST) + 2 * len(P_LIST) + len(A_LIST)
    assert TURN % NR == 0 and PRO % NR == 0

    class Stage:

        def __init__(self, first, b, names):
            self.first, self.b, self.names = first, b, names

        def slot(self, name):
            g = self.first + self.names.index(name)
            return g % NR, self.b * (TURN // NR) + g // NR

    def exists(c):
        return c is not None and not (isinstance(c, int) and c >= BATCH)

    def wait(eng, sem, value):
        if not (isinstance(value, int) and value <= 0):
            eng.wait_ge(sem, value)

    def alone(eng):
        eng.nop(nofuse=True)

    ctx = ExitStack()
    with ctx:
        def sb(name, shape, dt):
            return ctx.enter_context(nc.sbuf_tensor(name, shape, dt))

        def sem(name):
            return ctx.enter_context(nc.semaphore(name))

        q_stack = [sb(f"q_stack{p}", [P, 2, PAIRS, SEQ], f32r) for p in range(2)]
        k_stack = [sb(f"k_stack{p}", [P, PAIRS, SEQ], f32r) for p in range(2)]
        v_ones = [sb(f"v_ones{p}", [P, TILES, HEADS, VW], f32) for p in range(2)]
        probs = sb("probs", [P, NPB, SEQ], f32)
        o_cols = sb("o_cols", [P, GROUPS, SEQ], f32)
        split_a = sb("split_a", [P, 2, CH, SEQ], f32r)
        split_b = sb("split_b", [P, 2, CH, SEQ], f32r)
        xs = sb("xs", [P, 2, CH, SEQ], f32r)
        mix_k = sb("mix_k", [P, 2, CH, SEQ], f32r)
        x_cols = sb("x_cols", [P, CH, SEQ + 2], f32)
        gate = x_cols[:, :, 2:SEQ + 2]
        mixed = sb("mixed", [P, CH, SEQ], f32)
        relu_k = sb("relu_k", [P, CH, SEQ], f32)
        x_in = sb("x_in", [P, TILES, D], f32)
        rows = sb("rows", [P, TILES, D], f32)
        acc = [sb(f"acc{p}", [P, TILES, D], f32) for p in range(2)]
        weight = {n: sb(f"w_{n}", [P, 2, CH, D], f32r)
                  for n in ("q", "k", "v", "o", "fr", "fk", "fv")}
        ident = sb("ident", [P, P], f32)
        causal = sb("causal", [P, SEQ], f32)
        maxes = sb("maxes", [P, 2, PAIRS, TILES], f32)
        shifts = sb("shifts", [2 * PAIRS * TILES, P], f32)
        zeros = sb("zeros", [PAIRS * TILES, P], f32)
        ones = sb("ones", [PAIRS * TILES, P], f32)
        mus = sb("mus", [P, 2, CH], f32)
        one_minus_mus = sb("one_minus_mus", [P, 2, CH], f32)
        stats = sb("stats", [P, TILES, 6], f32)
        mean_var = sb("mean_var", [P, TILES, 2], f32)
        neg_mean = sb("neg_mean", [P, TILES], f32)
        var_eps = sb("var_eps", [P, TILES], f32)
        rstd = sb("rstd", [P, TILES], f32)
        minus_half = sb("minus_half", [P, TILES], f32)
        inv_den = sb("inv_den", [P, TILES, HEADS], f32)

        bank = [ctx.enter_context(nc.psum_tensor(f"bank{n}", [P, SEQ], f32)) for n in range(NR)]
        score = [ctx.enter_context(nc.psum_tensor(f"score{n}", [P, SEQ], f32)) for n in range(NSB)]
        attn = [ctx.enter_context(nc.psum_tensor(f"attn{n}", [P, SEQ], f32)) for n in range(2)]

        weights_in, mus_in, ones_in = sem("weights_in"), sem("mus_in"), sem("ones_in")
        cleared, consts_ready, setup_step = sem("cleared"), sem("consts_ready"), sem("setup_step")
        x_loaded, x_used = sem("x_loaded"), sem("x_used")
        bn_ready, moments_ready, ln_scalars, rstd_ready, rows_ready = (
            sem("bn_ready"), sem("moments_ready"), sem("ln_scalars"), sem("rstd_ready"), sem("rows_ready"))
        filled = [sem(f"filled{n}") for n in range(NR)]
        drained = [sem(f"drained{n}") for n in range(NR)]
        mix_scaled, mix_summed, mix_hi, mix_split = (
            sem("mix_scaled"), sem("mix_summed"), sem("mix_hi"), sem("mix_split"))
        x_copied, x_split, qk_hi, o_hi = sem("x_copied"), sem("x_split"), sem("qk_hi"), sem("o_hi")
        act_hi, squared, act_split = sem("act_hi"), sem("squared"), sem("act_split")
        inv_ready = sem("inv_ready")
        q_stacked, k_stacked, shift_zeroed, shift_in, stored = (
            sem("q_stacked"), sem("k_stacked"), sem("shift_zeroed"), sem("shift_in"), sem("stored"))
        score_filled, exp_done, masked, lot_done, o_copied = (
            sem("score_filled"), sem("exp_done"), sem("masked"), sem("lot_done"), sem("o_copied"))

        QD = KD = 16 * 6

        def schedule(do_ab, do_c):
            at = len(X_LIST)
            do_c(Stage(at, 0, P_LIST), None, 0, 0)
            do_ab(Stage(at + len(P_LIST), 0, A_LIST), None, 0, 1)
            do_c(Stage(at + len(P_LIST) + len(A_LIST), 0, P_LIST), None, 1, 1)

            def turn(b, parity):
                do_ab(Stage(PRO, b, A_LIST), b, b + 1, parity)
                do_c(Stage(PRO + len(A_LIST), b, C_LIST), b, b + 2, parity)

            turn(0, 0)
            turn(1, 1)
            return turn

        def epilogue(do_ab, do_c):
            last = BATCH - 2
            end = PRO + TURN * last
            names = [n for n in A_LIST if n not in X_LIST]
            do_ab(Stage(end, 0, names), last, last + 1, 0)
            do_c(Stage(end + len(names), 0, F_LIST), last, None, 0)
            do_ab(None, last + 1, None, 1)
            do_c(Stage(end + len(names) + len(F_LIST), 0, F_LIST), last + 1, None, 1)

        def run(eng, do_ab, do_c):
            turn = schedule(do_ab, do_c)
            with eng.Fori(1, (BATCH - 2) // 2) as i:
                turn(i * 2, 0)
                turn(i * 2 + 1, 1)
            epilogue(do_ab, do_c)

        block = ctx.enter_context(nc.Block())

        @block.sync
        def _(sp):
            for n, w in enumerate((wq_t, wk_t, wv_t, wo_t, fr_t, fk_t, fv_t)):
                sp.dma_start(probs[:, n, :], w).then_inc(weights_in, 16)
            sp.dma_start(mus[:, :, :], mu).then_inc(mus_in, 16)

            def load_x(b):
                sp.dma_start(x_in[:, :, :], x[bass.ds(b, 1), :, :].rearrange("b (t p) d -> p (b t) d", p=P)
                             ).then_inc(x_loaded, 16)

            load_x(0)
            sp.wait_ge(cleared, 3)
            for p in range(2):
                for par in range(2):
                    r = HALF * par + SHIFT_ROW
                    sp.dma_start(k_stack[p][r:r + 1, :, :].bitcast(f32), ones[:, :]).then_inc(ones_in, 16)

            def do_ab(st, b, c, parity):
                if c is None:
                    return
                if exists(c + 1):
                    sp.wait_ge(x_used, 2 * (c + 1))
                    load_x(c + 1)
                bank_n, uses = st.slot("turned")
                sp.wait_ge(drained[bank_n], uses + 1)
                for par in range(2):
                    r, rows_n = HALF * par + SHIFT_ROW, PAIRS * TILES
                    sp.dma_start(q_stack[1 - parity][r:r + 1, par, :, :].bitcast(f32),
                                 shifts[par * rows_n:(par + 1) * rows_n, :]).then_inc(shift_in, 16)

            def do_c(st, b, c, parity):
                if c is not None:
                    qs, ks = q_stack[parity], k_stack[parity]
                    if b is not None:
                        sp.wait_ge(score_filled, NU * (b + 1))
                        alone(sp)
                        sp.wait_ge(shift_in, 32 * (b + 1))
                    for names, src, terms, done in ((("q0", "q1"), split_a, (0, 0, 1), q_stacked),
                                                    (("k0", "k1"), split_b, (0, 1, 0), k_stacked)):
                        for name in names:
                            bank_n, uses = st.slot(name)
                            sp.wait_ge(drained[bank_n], uses + 1)
                        for par in range(2):
                            for n, part in enumerate(terms):
                                r = HALF * par + DH * n
                                dst = (qs[r:r + DH, par, :, :] if src is split_a else ks[r:r + DH, :, :])
                                sp.dma_start(dst.bitcast(f32),
                                             src[HALF * par:HALF * (par + 1), part, :, :].bitcast(f32)
                                             ).then_inc(done, 16)
                    for par in range(2):
                        r = HALF * par + SHIFT_ROW
                        sp.dma_start(qs[r:r + 1, par, :, :].bitcast(f32), zeros[:, :]).then_inc(shift_zeroed, 16)
                if b is not None:
                    bank_n, uses = st.slot("op1")
                    sp.wait_ge(drained[bank_n], uses + 1)
                    sp.dma_start(out[bass.ds(b, 1), :, :].rearrange("b (t p) d -> p (b t) d", p=P),
                                 acc[parity][:, :, :]).then_inc(stored, 16)

            run(sp, do_ab, do_c)
            sp.wait_ge(stored, 16 * BATCH)

        @block.gpsimd
        def _(pool):
            nc.gpsimd.memset(zeros[:, :], 0.0).then_inc(cleared, 1)
            nc.gpsimd.memset(ones[:, :], 1.0).then_inc(cleared, 1)
            nc.gpsimd.memset(minus_half[:, :], -0.5).then_inc(consts_ready, 1)
            nc.gpsimd.memset(ident[:, :], 1.0).then_inc(consts_ready, 1)
            nc.gpsimd.memset(causal[:, :], 0.0).then_inc(consts_ready, 1)
            pool.wait_ge(consts_ready, 3)
            nc.gpsimd.affine_select(out=ident[:, :], in_=ident[:, :], compare_op=ALU.is_equal, fill=0.0, base=0,
                                    pattern=[[-1, P]], channel_multiplier=1).then_inc(consts_ready, 1)
            last_tile = causal[:, SEQ - P:SEQ]
            nc.gpsimd.affine_select(out=last_tile, in_=last_tile, compare_op=ALU.is_ge, fill=MASKED, base=0,
                                    pattern=[[-1, P]], channel_multiplier=1).then_inc(consts_ready, 1)

            def ln_part(c, t, last_read):
                if t < 0:
                    pool.wait_ge(ln_scalars, 2 * (c + 1))
                    nc.gpsimd.tensor_tensor(rstd[:, :], var_eps[:, :], minus_half[:, :], ALU.pow).then_inc(rstd_ready, 1)
                    pool.wait_ge(rstd_ready, c + 1)
                    if last_read is not None:
                        pool.wait_ge(filled[last_read[0]], last_read[1] + 1)
                    alone(pool)
                else:
                    nc.gpsimd.tensor_scalar(rows[:, t, :], x_in[:, t, :], neg_mean[:, t:t + 1], rstd[:, t:t + 1],
                                            ALU.add, ALU.mult).then_inc(rows_ready, 1)

            def layernorm(c, last_read):
                for t in range(-1, TILES):
                    ln_part(c, t, last_read)

            def do_ab(st, b, c, parity):
                for n, (kind, _, _) in enumerate(UNITS):
                    if b is not None:
                        pool.wait_ge(exp_done, NU * b + n + 1)
                        alone(pool)
                        tile = probs[:, n % NPB, :]
                        if kind == 0:
                            view, pattern = tile[:, 0:P], [[1, P]]
                        else:
                            apart = SEQ - P if kind == 1 else SEQ // 2
                            view = tile.rearrange("p (a k) -> p a k", k=P)[:, 0::apart // P, :]
                            pattern = [[0, 2], [1, P]]
                        nc.gpsimd.affine_select(out=view, in_=view, compare_op=ALU.is_ge, fill=0.0, base=0,
                                                pattern=pattern, channel_multiplier=-1).then_inc(masked, 1)
                        if n in RESIDUAL_UNITS and exists(b + 1):
                            residual(b + 1, RESIDUAL_UNITS.index(n), 1 - parity, None if isinstance(b, int) and b == 0 else b)
                    if n in ROWS_UNITS and c is not None and exists(c + 1):
                        if b is None:
                            last = Stage(0, 0, X_LIST).slot("xT1")
                        elif isinstance(b, int) and b == 0:
                            last = Stage(len(X_LIST) + len(P_LIST), 0, A_LIST).slot("xT1")
                        else:
                            last = Stage(PRO + len(A_LIST) - TURN, b, C_LIST).slot("oc1")
                        ln_part(c + 1, ROWS_UNITS.index(n) - 1, last)
                    if n in SPLIT_UNITS and c is not None and exists(c + 1):
                        split_x(st, c + 1, SPLIT_UNITS.index(n))

            def split_x(st, c, m):
                bank_n, uses = st.slot(f"xT{m}")
                pool.wait_ge(drained[bank_n], uses + 1)
                nc.gpsimd.tensor_tensor(xs[:, 1, m, :], x_cols[:, m, 2:SEQ + 2], xs[:, 0, m, :].bitcast(f32),
                                        ALU.subtract).then_inc(x_split, 1)

            def residual(c, m, parity, earlier):
                if earlier is not None:
                    pool.wait_ge(stored, 16 * earlier)
                if isinstance(c, int) and c <= 1:
                    first = len(X_LIST) + c * (len(P_LIST) + len(A_LIST))
                    bank_n, uses = Stage(first, 0, P_LIST).slot(f"wv{m}")
                else:
                    bank_n, uses = Stage(PRO + len(A_LIST) - 2 * TURN, c, C_LIST).slot(f"wv{m}")
                pool.wait_ge(drained[bank_n], uses + 1)
                nc.gpsimd.tensor_tensor(acc[parity][:, 2 * m:2 * m + 2, :], gate[:, m, :].rearrange("p (t d) -> p t d", t=2),
                                        x_in[:, 2 * m:2 * m + 2, :], ALU.add).then_inc(x_used, 1)

            def do_c(st, b, c, parity):
                if c is None:
                    return
                for m in range(CH):
                    bank_n, uses = st.slot(f"kf{m}")
                    pool.wait_ge(drained[bank_n], uses + 1)
                    pool.wait_ge(mix_split, MIXES * c + CH + m + 1)
                    nc.gpsimd.tensor_tensor(mixed[:, m, :], relu_k[:, m, :], relu_k[:, m, :], ALU.mult
                                            ).then_inc(squared, 1)
                if isinstance(c, int) and c == 0:
                    for m in range(2):
                        residual(0, m, 0, None)

            layernorm(0, None)
            for m in range(CH):
                split_x(Stage(0, 0, X_LIST), 0, m)
            run(pool, do_ab, do_c)

        @block.scalar
        def _(act):
            def do_ab(st, b, c, parity):
                for n in range(NU):
                    if b is not None:
                        act.wait_ge(score_filled, NU * b + n + 1)
                        wait(act, lot_done, NL * b + (lot_of[n - NPB] + 1 if n >= NPB else lot_of[NU + n - NPB] + 1 - NL))
                        nc.scalar.activation(probs[:, n % NPB, :], score[n % NSB][:, :], ACT.Exp).then_inc(exp_done, 1)
                    if b is not None and n >= GU and n % GU == 5:
                        copy_out(b, n // GU - 1)
                    if n == XT_AT - 1 and c is not None and exists(c + 1):
                        turn_x(st, c + 1)
                if c is not None:
                    bank_n, uses = st.slot("turned")
                    act.wait_ge(filled[bank_n], uses + 1)
                    wait(act, shift_in, 32 * c)
                    nc.scalar.mul(shifts[:, :], bank[bank_n][0:2 * PAIRS * TILES, 0:P], -1.0
                                  ).then_inc(drained[bank_n], 1)
                if b is not None:
                    copy_out(b, GROUPS - 1)

            def turn_x(st, c):
                wait(act, x_used, 2 * c)
                for m in range(CH):
                    bank_n, uses = st.slot(f"xT{m}")
                    act.wait_ge(filled[bank_n], uses + 1)
                    nc.scalar.copy(x_cols[:, m, 2:SEQ + 2], bank[bank_n][:, :]).then_inc(x_copied, 1)
                    nc.scalar.copy(xs[:, 0, m, :], bank[bank_n][:, :]).then_inc(drained[bank_n], 1)

            def scale_before(c, w, m):
                at = MIXES * c + CH * (1 - w) + m
                wait(act, mix_split, at + 1 - CH)
                wait(act, x_copied, CH * c + m + 1)
                nc.scalar.activation(mixed[:, m, :], x_cols[:, m, 1:SEQ + 1], ACT.Copy,
                                     scale=one_minus_mus[:, w, m:m + 1]).then_inc(mix_scaled, 1)

            def mix_hi_part(c, w, m):
                if w == 0:
                    act.wait_ge(q_stacked, QD * (c + 1))
                act.wait_ge(mix_summed, MIXES * c + CH * (1 - w) + m + 1)
                nc.scalar.copy((mix_k if w else split_a)[:, 0, m, :], mixed[:, m, :]).then_inc(mix_hi, 1)

            def copy_out(b, g):
                act.wait_ge(lot_done, NL * b + 3 * (g + 1))
                nc.scalar.copy(o_cols[:, g, :], attn[g % 2][:, :]).then_inc(o_copied, 1)

            def do_c(st, b, c, parity):
                for name in st.names:
                    kind, m = name[:-1], int(name[-1])
                    if kind in ("ot", "op", "wv"):
                        continue
                    bank_n, uses = st.slot(name)
                    act.wait_ge(filled[bank_n], uses + 1)
                    src = bank[bank_n][:, :]
                    if kind == "q":
                        nc.scalar.mul(split_a[:, 0, m, :], src, SCALE).then_inc(qk_hi, 1)
                        scale_before(c, 1, m)
                    if kind == "k":
                        nc.scalar.copy(split_b[:, 0, m, :], src).then_inc(qk_hi, 1)
                        mix_hi_part(c, 1, m)
                    if kind == "v":
                        nc.scalar.copy(v_ones[parity][:, 2 * m:2 * m + 2, :, 0:DH],
                                       src.rearrange("p (t h d) -> p t h d", t=2, h=HEADS)
                                       ).then_inc(drained[bank_n], 1)
                        if m == 0:
                            scale_before(c, 0, 0)
                            scale_before(c, 0, 1)
                        else:
                            mix_hi_part(c, 0, 0)
                            mix_hi_part(c, 0, 1)
                    if kind == "kf":
                        wait(act, squared, CH * c)
                        nc.scalar.activation(relu_k[:, m, :], src, ACT.Relu).then_inc(drained[bank_n], 1)
                    if kind == "oc":
                        nc.scalar.copy(mix_k[:, 0, m, :], src).then_inc(o_hi, 1)
                    if name == "r1":
                        act.wait_ge(k_stacked, KD * (c + 1))
                        for half in range(CH):
                            kf_bank, kf_uses = st.slot(f"kf{half}")
                            act.wait_ge(drained[kf_bank], kf_uses + 1)
                            nc.scalar.activation(split_b[:, 0, half, :], relu_k[:, half, :], ACT.Square).then_inc(act_hi, 1)
                    if kind == "r":
                        nc.scalar.activation(gate[:, m, :], src, ACT.Tanh, scale=0.5).then_inc(drained[bank_n], 1)

            turn_x(Stage(0, 0, X_LIST), 0)
            run(act, do_ab, do_c)

        @block.vector
        def _(dve):
            steps = [0]

            def step(ins):
                steps[0] += 1
                ins.then_inc(setup_step, 1)
                dve.wait_ge(setup_step, steps[0])

            for p in range(2):
                step(nc.vector.memset(q_stack[p][:, :, :, :].bitcast(f32), 0.0))
                step(nc.vector.memset(k_stack[p][:, :, :].bitcast(f32), 0.0))
                step(nc.vector.memset(v_ones[p][:, :, :, :], 1.0))
                step(nc.vector.memset(attn[p][:, :], 0.0))
            nc.vector.memset(x_cols[:, :, 0:2], 0.0).then_inc(cleared, 1)

            dve.wait_ge(weights_in, 16 * 7)
            dve.wait_ge(mus_in, 16)
            step(nc.vector.tensor_scalar(one_minus_mus[:, :, :], mus[:, :, :], -1.0, 1.0, ALU.mult, ALU.add))
            step(nc.vector.tensor_scalar(probs[:, 6, :], probs[:, 6, :], 0.5, None, ALU.mult))

            def split(name, src):
                hi, lo = (weight[name][:, n, :, :] for n in range(2))
                src = src.rearrange("p (c d) -> p c d", c=CH)
                step(nc.vector.tensor_copy(hi, src))
                step(nc.vector.tensor_tensor(lo, src, hi.bitcast(f32), ALU.subtract))

            for n, name in enumerate(("q", "k", "v", "o", "fr", "fk", "fv")):
                split(name, probs[:, n, :])

            def ln_part(c, t):
                if t < TILES:
                    dve.wait_ge(x_loaded, 16 * (c + 1))
                    nc.vector.bn_stats(stats[:, t, :], x_in[:, t, :]).then_inc(bn_ready, 1)
                if t > 0:
                    dve.wait_ge(bn_ready, TILES * c + t)
                    alone(dve)
                    nc.vector.bn_aggr(mean_var[:, t - 1, :], stats[:, t - 1, :]).then_inc(moments_ready, 1)
                if t == TILES:
                    dve.wait_ge(moments_ready, TILES * (c + 1))
                    wait(dve, rows_ready, TILES * c)
                    nc.vector.tensor_scalar(neg_mean[:, :], mean_var[:, :, 0], -1.0, None, ALU.mult).then_inc(ln_scalars, 1)
                    nc.vector.tensor_scalar(var_eps[:, :], mean_var[:, :, 1], EPS, None, ALU.add).then_inc(ln_scalars, 1)

            def layernorm(c):
                for t in range(TILES + 1):
                    ln_part(c, t)

            def do_ab(st, b, c, parity):
                if c is not None:
                    for n, (kind, pair, par) in enumerate(UNITS):
                        bank_n, uses = st.slot(n)
                        dve.wait_ge(filled[bank_n], uses + 1)
                        alone(dve)
                        for at, pr, tile in max_parts(kind, par):
                            keys = (tile + 1) * P
                            part = bank[bank_n][:, at:at + keys]
                            ins = nc.vector.tensor_tensor_reduce(
                                out=part, in0=part, in1=causal[:, SEQ - keys:SEQ], scale=1.0, scalar=LOWEST,
                                op0=ALU.add, op1=ALU.max, accum_out=maxes[:, pr, pair, tile:tile + 1])
                        ins.then_inc(drained[bank_n], 1)
                        if n in LN_UNITS and exists(c + 1):
                            ln_part(c + 1, LN_UNITS.index(n))

            def mix(c, w, m):
                dve.wait_ge(mix_scaled, MIXES * c + CH * (1 - w) + m + 1)
                nc.vector.scalar_tensor_tensor(mixed[:, m, :], x_cols[:, m, 2:SEQ + 2], mus[:, w, m:m + 1], mixed[:, m, :],
                                               ALU.mult, ALU.add).then_inc(mix_summed, 1)

            def mix_lo_part(c, w, m):
                dst = mix_k if w else split_a
                dve.wait_ge(mix_hi, MIXES * c + CH * (1 - w) + m + 1)
                nc.vector.tensor_tensor(dst[:, 1, m, :], mixed[:, m, :], dst[:, 0, m, :].bitcast(f32), ALU.subtract
                                        ).then_inc(mix_split, 1)

            def do_c(st, b, c, parity):
                for name in st.names:
                    kind, m = name[:-1], int(name[-1])
                    bank_n, uses = st.slot(name)
                    src = bank[bank_n][:, :]
                    if kind == "q":
                        dve.wait_ge(qk_hi, 2 * CH * c + m + 1)
                        nc.vector.scalar_tensor_tensor(split_a[:, 1, m, :], src, SCALE, split_a[:, 0, m, :].bitcast(f32),
                                                       ALU.mult, ALU.subtract).then_inc(drained[bank_n], 1)
                        if m == 1:
                            mix(c, 1, 0)
                    if kind == "k":
                        dve.wait_ge(qk_hi, 2 * CH * c + CH + m + 1)
                        nc.vector.tensor_tensor(split_b[:, 1, m, :], src, split_b[:, 0, m, :].bitcast(f32),
                                                ALU.subtract).then_inc(drained[bank_n], 1)
                        if m == 0:
                            mix(c, 1, 1)
                        else:
                            mix_lo_part(c, 1, 0)
                    if name == "v0":
                        mix_lo_part(c, 1, 1)
                    if name == "v1":
                        mix(c, 0, 0)
                        mix(c, 0, 1)
                    if kind == "ot":
                        dve.wait_ge(filled[bank_n], uses + 1)
                        per_head = src.rearrange("p (h d) -> p h d", h=HEADS)
                        nc.vector.reciprocal(inv_den[:, m, :], per_head[:, :, DH]).then_inc(inv_ready, 1)
                        dve.wait_ge(inv_ready, TILES * b + m + 1)
                        nc.vector.tensor_tensor(rows[:, m, :].rearrange("p (h d) -> p h d", h=HEADS), per_head[:, :, 0:DH],
                                                inv_den[:, m, :].unsqueeze(2).to_broadcast([P, HEADS, DH]), ALU.mult
                                                ).then_inc(drained[bank_n], 1)
                    if name == "kf1":
                        mix_lo_part(c, 0, 0)
                        mix_lo_part(c, 0, 1)
                    if name == "r1":
                        for half in range(CH):
                            dve.wait_ge(act_hi, CH * c + half + 1)
                            dve.wait_ge(squared, CH * c + half + 1)
                            nc.vector.tensor_tensor(split_b[:, 1, half, :], mixed[:, half, :],
                                                    split_b[:, 0, half, :].bitcast(f32), ALU.subtract).then_inc(act_split, 1)
                    if kind == "oc":
                        dve.wait_ge(o_hi, CH * b + m + 1)
                        nc.vector.tensor_tensor(mix_k[:, 1, m, :], src, mix_k[:, 0, m, :].bitcast(f32),
                                                ALU.subtract).then_inc(drained[bank_n], 1)
                    if kind == "op":
                        dve.wait_ge(filled[bank_n], uses + 1)
                        dve.wait_ge(x_used, 2 * (b + 1))
                        nc.vector.tensor_tensor(acc[parity][:, 2 * m:2 * m + 2, :], src.rearrange("p (t d) -> p t d", t=2),
                                                acc[parity][:, 2 * m:2 * m + 2, :], ALU.add).then_inc(drained[bank_n], 1)
                    if kind == "wv":
                        dve.wait_ge(filled[bank_n], uses + 1)
                        r_bank, r_uses = st.slot(f"r{m}")
                        dve.wait_ge(drained[r_bank], r_uses + 1)
                        nc.vector.scalar_tensor_tensor(gate[:, m, :], gate[:, m, :], 1.0, src, ALU.add, ALU.mult
                                                       ).then_inc(drained[bank_n], 1)

            layernorm(0)
            run(dve, do_ab, do_c)

        @block.tensor
        def _(pe):
            pe.wait_ge(consts_ready, 5)
            pe.wait_ge(cleared, 3)
            pe.wait_ge(ones_in, 16 * 4)
            pe.wait_ge(setup_step, 1)

            def open_slot(st, name):
                bank_n, uses = st.slot(name)
                wait(pe, drained[bank_n], uses)
                return bank_n, bank[bank_n]

            def maxima(st, c, n, parity):
                kind, pair, par = UNITS[n]
                qs, ks = q_stack[parity], k_stack[parity]
                bank_n, dst = open_slot(st, n)
                for at, pr, tile in max_parts(kind, par):
                    keys = (tile + 1) * P
                    ins = nc.tensor.matmul(dst[:, at:at + keys], qs[:, pr, pair, tile * P:(tile + 1) * P],
                                           ks[:, pair, 0:keys], start=True, stop=True)
                ins.then_inc(filled[bank_n], 1)

            def scores(b, n, parity):
                kind, pair, par = UNITS[n]
                qs, ks = q_stack[parity], k_stack[parity]
                dst = score[n % NSB]
                before = n - NSB if n >= NSB else NU - 1 - (NU - 1 - n) % NSB - NU
                wait(pe, exp_done, NU * b + before + 1)
                if kind == 0:
                    parts = [(0, par, 0)]
                if kind == 1:
                    parts = [(0, par, 1), (SEQ - P, par, 3)]
                if kind == 2:
                    parts = [(0, 0, 2), (SEQ // 2, 1, 2)]
                for at, pr, tile in parts:
                    queries = SEQ - tile * P
                    ins = nc.tensor.matmul(dst[:, at:at + queries], ks[:, pair, tile * P:(tile + 1) * P],
                                           qs[:, pr, pair, tile * P:SEQ], start=True, stop=True)
                ins.then_inc(score_filled, 1)

            def lot(b, n, parity):
                first, end = LOTS[n]
                g = n // 3
                if n % 3 == 0:
                    wait(pe, o_copied, GROUPS * b + g - 1)
                pe.wait_ge(masked, NU * b + end)
                todo = []
                for u in range(first, end):
                    kind, pair, par = UNITS[u]
                    if kind == 0:
                        todo += [(0, u, pair, par, 0, 0)]
                    if kind == 1:
                        todo += [(0, u, pair, par, 0, 1), (1, u, pair, par, SEQ - P, 3)]
                    if kind == 2:
                        todo += [(0, u, pair, 0, 0, 2), (0, u, pair, 1, SEQ // 2, 2)]
                todo.sort(key=lambda x: x[0])
                for _, u, pair, par, at, tile in todo:
                    quad = (pair % 2) * 2 + par
                    head = 4 * g + quad
                    queries = SEQ - tile * P
                    ins = nc.tensor.matmul(attn[g % 2][32 * quad:32 * quad + VW, tile * P:SEQ],
                                           v_ones[parity][:, tile, head, :], probs[:, u % NPB, at:at + queries],
                                           start=(tile == 0), stop=(tile == 2), skip_group_check=True)
                ins.then_inc(lot_done, 1)

            def do_ab(st, b, c, parity):
                if c is not None:
                    pe.wait_ge(q_stacked, QD * (c + 1))
                    pe.wait_ge(k_stacked, KD * (c + 1))
                    pe.wait_ge(shift_zeroed, 32 * (c + 1))
                if b is not None:
                    pe.wait_ge(shift_in, 32 * (b + 1))
                todo = list(range(NL))
                for n in range(NU):
                    if n == XT_AT and c is not None and exists(c + 1):
                        turn_x(st, c + 1)
                    if c is not None:
                        maxima(st, c, n, 1 - parity)
                    if b is not None:
                        scores(b, n, parity)
                        if todo and LOTS[todo[0]][1] - 1 + LAG <= n:
                            lot(b, todo.pop(0), parity)
                if c is not None:
                    bank_n, dst = open_slot(st, "turned")
                    last, uses = st.slot(NU - 1)
                    pe.wait_ge(drained[last], uses + 1)
                    alone(pe)
                    nc.tensor.transpose(dst[0:2 * PAIRS * TILES, 0:P], maxes[:, :, :, :].rearrange("p a b c -> p (a b c)"),
                                        ident[:, :]).then_inc(filled[bank_n], 1)
                if b is not None:
                    for n in todo:
                        lot(b, n, parity)

            def turn_x(st, c):
                for m in range(CH):
                    bank_n, dst = open_slot(st, f"xT{m}")
                    pe.wait_ge(rows_ready, TILES * (c + 1))
                    alone(pe)
                    for t in range(TILES):
                        ins = nc.tensor.transpose(dst[:, t * P:(t + 1) * P], rows[:, t, m * P:(m + 1) * P], ident[:, :])
                    ins.then_inc(filled[bank_n], 1)

            def products(dst, pairs):
                for n, (lhs, rhs) in enumerate(pairs):
                    ins = nc.tensor.matmul(dst, lhs, rhs, start=(n == 0), stop=(n == len(pairs) - 1))
                return ins

            SPLIT = ((0, 0), (0, 1), (1, 0))

            def columns(dst, m, a, w):
                return products(dst[:, :], [(w[:, pw, c, m * P:(m + 1) * P], a(pa, c)) for pa, pw in SPLIT for c in range(CH)])

            def tokens(dst, m, a, w):
                for i in range(2):
                    cut = slice((2 * m + i) * P, (2 * m + i + 1) * P)
                    ins = products(dst[:, i * D:(i + 1) * D],
                                   [(a(pa, c)[:, cut], w[:, pw, c, :]) for pa, pw in SPLIT for c in range(CH)])
                return ins

            def part_x(part, c):
                return xs[:, part, c, :]

            def part_k(part, c):
                return mix_k[:, part, c, :]

            def part_a(part, c):
                return split_a[:, part, c, :]

            def part_b(part, c):
                return split_b[:, part, c, :]

            def do_c(st, b, c, parity):
                for name in st.names:
                    kind, m = name[:-1], int(name[-1])
                    bank_n, dst = open_slot(st, name)
                    if kind in ("q", "k"):
                        if name == "q0":
                            pe.wait_ge(x_split, CH * (c + 1))
                        ins = columns(dst, m, part_x, weight[kind])
                    if kind == "v":
                        ins = tokens(dst, m, part_x, weight["v"])
                    if kind == "kf":
                        pe.wait_ge(mix_split, MIXES * c + CH)
                        ins = columns(dst, m, part_k, weight["fk"])
                    if kind == "r":
                        pe.wait_ge(mix_split, MIXES * (c + 1))
                        ins = tokens(dst, m, part_a, weight["fr"])
                    if kind == "ot":
                        wait(pe, o_copied, GROUPS * (b + 1))
                        for g in range(GROUPS):
                            ins = nc.tensor.transpose(dst[:, g * P:(g + 1) * P], o_cols[:, g, m * P:(m + 1) * P], ident[:, :])
                    if kind == "oc":
                        for t in range(TILES):
                            if m == 0:
                                t_bank, uses = st.slot(f"ot{t}")
                                pe.wait_ge(drained[t_bank], uses + 1)
                            ins = nc.tensor.transpose(dst[:, t * P:(t + 1) * P], rows[:, t, m * P:(m + 1) * P], ident[:, :])
                    if kind == "op":
                        if m == 0:
                            for o_name in ("oc0", "oc1"):
                                o_bank, uses = st.slot(o_name)
                                pe.wait_ge(drained[o_bank], uses + 1)
                        ins = tokens(dst, m, part_k, weight["o"])
                    if kind == "wv":
                        pe.wait_ge(act_split, CH * (c + 1))
                        ins = tokens(dst, m, part_b, weight["fv"])
                    ins.then_inc(filled[bank_n], 1)

            turn_x(Stage(0, 0, X_LIST), 0)
            run(pe, do_ab, do_c)


def kernel(L0_attn_X, L0_attn_q_proj, L0_attn_k_proj, L0_attn_v_proj, L0_attn_o_proj,
           L0_ffn_W_r, L0_ffn_W_k, L0_ffn_W_v, L0_ffn_mu_r, L0_ffn_mu_k):
    import numpy as np
    import concourse.bacc as bacc
    from concourse.bass_utils import run_bass_kernel_spmd

    D, DH, P = 256, 16, 128

    def chunks(w):
        return np.ascontiguousarray(w.reshape(D // P, P, D).transpose(1, 0, 2).reshape(P, -1))

    def arr(a):
        return np.asarray(a)

    def for_stack(w):
        return arr(w).reshape(2, 4, 2, DH, D).transpose(4, 0, 2, 3, 1).reshape(D, D)

    data = {
        "x": arr(L0_attn_X),
        "wq_t": chunks(for_stack(L0_attn_q_proj)),
        "wk_t": chunks(for_stack(L0_attn_k_proj)),
        "wv_t": chunks(arr(L0_attn_v_proj).reshape(2, 4, 2, DH, D).transpose(4, 1, 0, 2, 3).reshape(D, D)),
        "wo_t": chunks(arr(L0_attn_o_proj).reshape(D, 2, 4, 2, DH).transpose(2, 1, 3, 4, 0).reshape(D, D)),
        "fr_t": chunks(arr(L0_ffn_W_r).T),
        "fk_t": chunks(arr(L0_ffn_W_k).T),
        "fv_t": chunks(arr(L0_ffn_W_v).T),
        "mu": np.ascontiguousarray(np.stack([arr(L0_ffn_mu_r), arr(L0_ffn_mu_k)]).reshape(2, D // P, P).transpose(2, 0, 1)),
    }
    nc = bacc.Bacc("TRN2", target_bir_lowering=False, num_devices=1, dynamic_dma_scratch_size=1024)
    args = {n: nc.dram_tensor(n, a.shape, mybir.dt.from_np(a.dtype), kind="ExternalInput").ap() for n, a in data.items()}
    out = nc.dram_tensor("out", data["x"].shape, mybir.dt.float32, kind="ExternalOutput").ap()
    attention_and_channel_mix(nc, **args, out=out)
    got = run_bass_kernel_spmd(nc, [data], core_ids=[0])
    return got.results[0]["out"]
```

```python
import concourse.bass as bass
from concourse import mybir
from contextlib import ExitStack


def attention_and_channel_mix(
    nc: bass.Bass,
    x: bass.AP,
    wq_t: bass.AP,
    wk_t: bass.AP,
    wv_t: bass.AP,
    wo_t: bass.AP,
    fr_t: bass.AP,
    fk_t: bass.AP,
    fv_t: bass.AP,
    mu: bass.AP,
    out: bass.AP,
):
    f32 = mybir.dt.float32
    f32r = mybir.dt.float32r
    ALU = mybir.AluOpType
    ACT = mybir.ActivationFunctionType
    AX = mybir.AxisListType.X

    BATCH, SEQ, D = x.shape
    P = 128
    HEADS = 16
    DH = D // HEADS
    TILES = SEQ // P
    CH = D // P
    PAIRS = HEADS // 2
    GROUPS = 4
    HALF = P // 2
    SHIFT_ROW = 3 * DH
    VW = DH + 1
    SCALE = float(DH) ** -0.5
    EPS = 1e-5
    MASKED = -1.0e38
    LOWEST = -3.4e38

    UNITS = []
    for g in range(GROUPS):
        heads4 = [(pair, par) for pair in (2 * g, 2 * g + 1) for par in range(2)]
        UNITS += [(0, pair, par) for pair, par in heads4]
        UNITS += [(1, pair, par) for pair, par in heads4]
        UNITS += [(2, pair, None) for pair in (2 * g, 2 * g + 1)]
    NU = len(UNITS)
    GU = NU // GROUPS
    def max_parts(kind, par):
        return {0: [(0, par, 3)], 1: [(0, par, 2), (SEQ - P, par, 0)], 2: [(0, 0, 1), (SEQ // 2, 1, 1)]}[kind]

    LOTS = [(g * GU + a, g * GU + z) for g in range(GROUPS) for a, z in ((0, 4), (4, 8), (8, 10))]
    NL = len(LOTS)
    LAG = 4
    AHEAD = 1
    NPB = 8
    RESIDUAL_UNITS = [3, 5, 8, 10]
    LN_UNITS = [17, 18, 20, 21, 23]
    ROWS_UNITS = [24, 27, 28, 29, 31]
    SPLIT_UNITS = [35, 39]
    FINISH_UNITS = {1: "ot0", 3: "ot1", 5: "ot2", 7: "ot3", 9: "oc0", 11: "oc1", 14: "op0", 16: "op1"}
    FINISH_HI_UNITS = {11: "oc0", 13: "oc1"}
    COPY_AT = 3
    NSB = 3
    lot_of = [n for n, (a, z) in enumerate(LOTS) for _ in range(a, z)]

    NR = 4
    MIXES = 2 * CH
    XT_AT = NU - 5
    A_LIST = [*range(XT_AT), "xT0", "xT1", *range(XT_AT, NU), "turned"]
    X_LIST = ["xT0", "xT1"]
    P_LIST = ["q0", "q1", "k0", "k1", "v0", "v1", "kf0", "kf1", "r0", "r1", "wv0", "wv1"]
    F_LIST = ["ot0", "ot1", "ot2", "ot3", "oc0", "oc1", "op0", "op1"]
    C_LIST = ["q0", "q1", "k0", "k1", "ot0", "v0", "ot1", "v1", "ot2", "kf0", "ot3",
              "kf1", "oc0", "r0", "oc1", "r1", "op0", "op1", "wv0", "wv1"]
    USED = len(A_LIST) + len(C_LIST)
    TURN = -(-USED // NR) * NR
    PRO = len(X_LIST) + 2 * len(P_LIST) + len(A_LIST)

    def uses_before(g):
        return sum(1 for x in range(g % NR, g, NR) if x < PRO or (x - PRO) % TURN < USED)

    class Stage:

        def __init__(self, first, b, names):
            self.first, self.b, self.names = first, b, names

        def slot(self, name):
            g = self.first + self.names.index(name)
            if isinstance(self.b, int):
                return g % NR, uses_before(g + TURN * self.b)
            a_turn = uses_before(g + 3 * TURN) - uses_before(g + 2 * TURN)
            return g % NR, self.b * a_turn + (uses_before(g + 2 * TURN) - 2 * a_turn)

    def exists(c):
        return c is not None and not (isinstance(c, int) and c >= BATCH)

    def wait(eng, sem, value):
        if not (isinstance(value, int) and value <= 0):
            eng.wait_ge(sem, value)

    def alone(eng):
        eng.nop(nofuse=True)

    ctx = ExitStack()
    with ctx:
        def sb(name, shape, dt):
            return ctx.enter_context(nc.sbuf_tensor(name, shape, dt))

        def sem(name):
            return ctx.enter_context(nc.semaphore(name))

        q_stack = [sb(f"q_stack{p}", [P, 2, PAIRS, SEQ], f32r) for p in range(2)]
        k_stack = [sb(f"k_stack{p}", [P, PAIRS, SEQ], f32r) for p in range(2)]
        v_ones = [sb(f"v_ones{p}", [P, TILES, HEADS, VW], f32) for p in range(2)]
        probs = sb("probs", [P, NPB, SEQ], f32)
        o_cols = sb("o_cols", [P, GROUPS, SEQ], f32)
        split_a = sb("split_a", [P, 2, CH, SEQ], f32r)
        split_b = sb("split_b", [P, 2, CH, SEQ], f32r)
        xs = sb("xs", [P, 2, CH, SEQ], f32r)
        mix_k = sb("mix_k", [P, 2, CH, SEQ], f32r)
        x_cols = sb("x_cols", [P, CH, SEQ + 2], f32)
        gate = x_cols[:, :, 2:SEQ + 2]
        mixed = sb("mixed", [P, CH, SEQ], f32)
        relu_k = sb("relu_k", [P, CH, SEQ], f32)
        x_in = sb("x_in", [P, TILES, D], f32)
        rows = sb("rows", [P, TILES, D], f32)
        acc = [sb(f"acc{p}", [P, TILES, D], f32) for p in range(2)]
        weight = {n: sb(f"w_{n}", [P, 2, CH, D], f32r)
                  for n in ("q", "k", "v", "fk", "fr", "fv", "o")}
        ident = sb("ident", [P, P], f32)
        causal = sb("causal", [P, SEQ], f32)
        maxes = sb("maxes", [P, 2, PAIRS, TILES], f32)
        shifts = sb("shifts", [2 * PAIRS * TILES, P], f32)
        zeros = sb("zeros", [PAIRS * TILES, P], f32)
        ones = sb("ones", [PAIRS * TILES, P], f32)
        mus = sb("mus", [P, 2, CH], f32)
        one_minus_mus = sb("one_minus_mus", [P, 2, CH], f32)
        stats = sb("stats", [P, TILES, 6], f32)
        mean_var = sb("mean_var", [P, TILES, 2], f32)
        neg_mean = sb("neg_mean", [P, TILES], f32)
        var_eps = sb("var_eps", [P, TILES], f32)
        rstd = sb("rstd", [P, TILES], f32)
        minus_half = sb("minus_half", [P, TILES], f32)
        inv_den = sb("inv_den", [P, TILES, HEADS], f32)

        bank = [ctx.enter_context(nc.psum_tensor(f"bank{n}", [P, SEQ], f32)) for n in range(NR)]
        score = [ctx.enter_context(nc.psum_tensor(f"score{n}", [P, SEQ], f32)) for n in range(NSB)]
        attn = ctx.enter_context(nc.psum_tensor("attn", [P, SEQ], f32))

        weight_in = {n: sem(f"w_{n}_in") for n in weight}
        weights_hi, weights_split = sem("weights_hi"), sem("weights_split")
        mus_in, mus_ready, consts_ready = sem("mus_in"), sem("mus_ready"), sem("consts_ready")
        q_cleared, k_cleared, v_cleared = (
            [sem(f"{n}_cleared{p}") for p in range(2)] for n in ("q", "k", "v"))
        attn_cleared, x_cols_cleared = sem("attn_cleared"), sem("x_cols_cleared")
        ones_in = [sem(f"ones_in{p}") for p in range(2)]
        x_loaded, x_used = sem("x_loaded"), sem("x_used")
        bn_ready, moments_ready, ln_scalars, rstd_ready, rows_ready = (
            sem("bn_ready"), sem("moments_ready"), sem("ln_scalars"), sem("rstd_ready"), sem("rows_ready"))
        filled = [sem(f"filled{n}") for n in range(NR)]
        drained = [sem(f"drained{n}") for n in range(NR)]
        mix_scaled, mix_summed, mix_hi, mix_split = (
            sem("mix_scaled"), sem("mix_summed"), sem("mix_hi"), sem("mix_split"))
        x_copied, x_split, qk_hi, o_hi = sem("x_copied"), sem("x_split"), sem("qk_hi"), sem("o_hi")
        act_hi, squared, act_split = sem("act_hi"), sem("squared"), sem("act_split")
        inv_ready = sem("inv_ready")
        q_stacked, k_stacked, shift_zeroed, shift_in, stored = (
            sem("q_stacked"), sem("k_stacked"), sem("shift_zeroed"), sem("shift_in"), sem("stored"))
        score_filled, exp_done, masked, lot_done, o_copied = (
            sem("score_filled"), sem("exp_done"), sem("masked"), sem("lot_done"), sem("o_copied"))

        QD = KD = 16 * 6

        def schedule(do_ab, do_c):
            at = len(X_LIST)
            do_c(Stage(at, 0, P_LIST), None, 0, 0)
            do_ab(Stage(at + len(P_LIST), 0, A_LIST), None, 0, 1)
            do_c(Stage(at + len(P_LIST) + len(A_LIST), 0, P_LIST), None, 1, 1)

            def turn(b, parity):
                do_ab(Stage(PRO, b, A_LIST), b, b + 1, parity)
                do_c(Stage(PRO + len(A_LIST), b, C_LIST), b, b + 2, parity)

            turn(0, 0)
            turn(1, 1)
            return turn

        def epilogue(do_ab, do_c):
            last = BATCH - 2
            end = PRO + TURN * last
            names = [n for n in A_LIST if n not in X_LIST]
            do_ab(Stage(end, 0, names), last, last + 1, 0)
            do_ab(None, last + 1, None, 1, Stage(end + len(names), 0, F_LIST))
            do_c(Stage(end + len(names) + len(F_LIST), 0, F_LIST), last + 1, None, 1)

        def run(eng, do_ab, do_c):
            turn = schedule(do_ab, do_c)
            with eng.Fori(1, (BATCH - 2) // 2) as i:
                turn(i * 2, 0)
                turn(i * 2 + 1, 1)
            epilogue(do_ab, do_c)

        block = ctx.enter_context(nc.Block())

        @block.sync
        def _(sp):
            def load_x(b):
                sp.dma_start(x_in[:, :, :], x[bass.ds(b, 1), :, :].rearrange("b (t p) d -> p (b t) d", p=P)
                             ).then_inc(x_loaded, 16)

            load_x(0)
            for n, (name, w) in enumerate(zip(weight, (wq_t, wk_t, wv_t, fk_t, fr_t, fv_t, wo_t))):
                sp.dma_start(probs[:, n, :], w).then_inc(weight_in[name], 16)
                if n == 1:
                    sp.dma_start(mus[:, :, :], mu).then_inc(mus_in, 16)

            def fill_ones(p):
                sp.wait_ge(consts_ready, 6)
                sp.wait_ge(k_cleared[p], 1)
                for par in range(2):
                    r = HALF * par + SHIFT_ROW
                    sp.dma_start(k_stack[p][r:r + 1, :, :].bitcast(f32), ones[:, :]).then_inc(ones_in[p], 16)
                sp.wait_ge(q_cleared[p], 2)

            def do_ab(st, b, c, parity, finish=None):
                if finish is not None:
                    do_c(finish, b - 1, None, 1 - parity)
                if c is None:
                    return
                if exists(c + 1):
                    sp.wait_ge(x_used, TILES * (c + 1))
                    load_x(c + 1)
                bank_n, uses = st.slot("turned")
                sp.wait_ge(drained[bank_n], uses + 1)
                for par in range(2):
                    r, rows_n = HALF * par + SHIFT_ROW, PAIRS * TILES
                    sp.dma_start(q_stack[1 - parity][r:r + 1, par, :, :].bitcast(f32),
                                 shifts[par * rows_n:(par + 1) * rows_n, :]).then_inc(shift_in, 16)

            def do_c(st, b, c, parity):
                if isinstance(c, int) and c <= 1:
                    fill_ones(c)
                if c is not None:
                    qs, ks = q_stack[parity], k_stack[parity]
                    if b is not None:
                        sp.wait_ge(score_filled, NU * (b + 1))
                        alone(sp)
                        sp.wait_ge(shift_in, 32 * (b + 1))
                        alone(sp)
                    for names, src, terms, done in ((("q0", "q1"), split_a, (0, 0, 1), q_stacked),
                                                    (("k0", "k1"), split_b, (0, 1, 0), k_stacked)):
                        for name in names:
                            bank_n, uses = st.slot(name)
                            sp.wait_ge(drained[bank_n], uses + 1)
                            alone(sp)
                        for par in range(2):
                            for n, part in enumerate(terms):
                                r = HALF * par + DH * n
                                dst = (qs[r:r + DH, par, :, :] if src is split_a else ks[r:r + DH, :, :])
                                sp.dma_start(dst.bitcast(f32),
                                             src[HALF * par:HALF * (par + 1), part, :, :].bitcast(f32)
                                             ).then_inc(done, 16)
                    for par in range(2):
                        r = HALF * par + SHIFT_ROW
                        sp.dma_start(qs[r:r + 1, par, :, :].bitcast(f32), zeros[:, :]).then_inc(shift_zeroed, 16)
                if b is not None:
                    bank_n, uses = st.slot("op1")
                    sp.wait_ge(drained[bank_n], uses + 1)
                    sp.dma_start(out[bass.ds(b, 1), :, :].rearrange("b (t p) d -> p (b t) d", p=P),
                                 acc[parity][:, :, :]).then_inc(stored, 16)

            run(sp, do_ab, do_c)
            sp.wait_ge(stored, 16 * BATCH)

        @block.gpsimd
        def _(pool):
            nc.gpsimd.memset(ident[:, :], 1.0).then_inc(consts_ready, 1)
            nc.gpsimd.memset(minus_half[:, :], -0.5).then_inc(consts_ready, 1)
            nc.gpsimd.memset(zeros[:, :], 0.0).then_inc(consts_ready, 1)
            nc.gpsimd.memset(ones[:, :], 1.0).then_inc(consts_ready, 1)
            nc.gpsimd.memset(causal[:, :], 0.0).then_inc(consts_ready, 1)
            pool.wait_ge(consts_ready, 5)
            nc.gpsimd.affine_select(out=ident[:, :], in_=ident[:, :], compare_op=ALU.is_equal, fill=0.0, base=0,
                                    pattern=[[-1, P]], channel_multiplier=1).then_inc(consts_ready, 1)
            last_tile = causal[:, SEQ - P:SEQ]
            nc.gpsimd.affine_select(out=last_tile, in_=last_tile, compare_op=ALU.is_ge, fill=MASKED, base=0,
                                    pattern=[[-1, P]], channel_multiplier=1).then_inc(consts_ready, 1)

            def clear_q(p, part):
                nc.gpsimd.memset(q_stack[p][:, part, :, :].bitcast(f32), 0.0).then_inc(q_cleared[p], 1)

            def ln_part(c, t, last_read):
                if t < 0:
                    pool.wait_ge(ln_scalars, 2 * (c + 1))
                    nc.gpsimd.tensor_tensor(rstd[:, :], var_eps[:, :], minus_half[:, :], ALU.pow).then_inc(rstd_ready, 1)
                    pool.wait_ge(rstd_ready, c + 1)
                    if last_read is not None:
                        pool.wait_ge(filled[last_read[0]], last_read[1] + 1)
                    alone(pool)
                else:
                    nc.gpsimd.tensor_scalar(rows[:, t, :], x_in[:, t, :], neg_mean[:, t:t + 1], rstd[:, t:t + 1],
                                            ALU.add, ALU.mult).then_inc(rows_ready, 1)

            def layernorm(c, last_read):
                for t in range(-1, TILES):
                    ln_part(c, t, last_read)

            def do_ab(st, b, c, parity, finish=None):
                if b is None:
                    for part in range(2):
                        clear_q(1, part)
                    nc.gpsimd.memset(k_stack[1][:, :, :].bitcast(f32), 0.0).then_inc(k_cleared[1], 1)
                    nc.gpsimd.memset(v_ones[1][:, :, :, :], 1.0).then_inc(v_cleared[1], 1)
                for n, (kind, _, _) in enumerate(UNITS):
                    if b is not None:
                        pool.wait_ge(exp_done, NU * b + n + 1)
                        alone(pool)
                        tile = probs[:, n % NPB, :]
                        if kind == 0:
                            view, pattern = tile[:, 0:P], [[1, P]]
                        else:
                            apart = SEQ - P if kind == 1 else SEQ // 2
                            view = tile.rearrange("p (a k) -> p a k", k=P)[:, 0::apart // P, :]
                            pattern = [[0, 2], [1, P]]
                        nc.gpsimd.affine_select(out=view, in_=view, compare_op=ALU.is_ge, fill=0.0, base=0,
                                                pattern=pattern, channel_multiplier=-1).then_inc(masked, 1)
                        if n in RESIDUAL_UNITS and exists(b + 1):
                            residual(b + 1, RESIDUAL_UNITS.index(n), 1 - parity, None if isinstance(b, int) and b == 0 else b)
                    if n in ROWS_UNITS and c is not None and exists(c + 1):
                        if b is None:
                            last = Stage(0, 0, X_LIST).slot("xT1")
                        elif isinstance(b, int) and b == 0:
                            last = Stage(len(X_LIST) + len(P_LIST), 0, A_LIST).slot("xT1")
                        else:
                            last = Stage(PRO + len(A_LIST) - TURN, b, C_LIST).slot("oc1")
                        ln_part(c + 1, ROWS_UNITS.index(n) - 1, last)
                    if n in SPLIT_UNITS and c is not None and exists(c + 1):
                        split_x(st, c + 1, SPLIT_UNITS.index(n))

            def split_x(st, c, m):
                bank_n, uses = st.slot(f"xT{m}")
                pool.wait_ge(drained[bank_n], uses + 1)
                nc.gpsimd.tensor_tensor(xs[:, 1, m, :], x_cols[:, m, 2:SEQ + 2], xs[:, 0, m, :].bitcast(f32),
                                        ALU.subtract).then_inc(x_split, 1)

            def residual(c, t, parity, earlier):
                m, i = t // 2, t % 2
                if earlier is not None:
                    pool.wait_ge(stored, 16 * earlier)
                if isinstance(c, int) and c <= 1:
                    first = len(X_LIST) + c * (len(P_LIST) + len(A_LIST))
                    bank_n, uses = Stage(first, 0, P_LIST).slot(f"wv{m}")
                else:
                    bank_n, uses = Stage(PRO + len(A_LIST) - 2 * TURN, c, C_LIST).slot(f"wv{m}")
                pool.wait_ge(drained[bank_n], uses + 1)
                nc.gpsimd.tensor_tensor(acc[parity][:, t, :], gate[:, m, i * D:(i + 1) * D], x_in[:, t, :], ALU.add
                                        ).then_inc(x_used, 1)

            def do_c(st, b, c, parity):
                if c is None:
                    return
                for m in range(CH):
                    bank_n, uses = st.slot(f"kf{m}")
                    pool.wait_ge(drained[bank_n], uses + 1)
                    pool.wait_ge(mix_split, MIXES * c + CH + m + 1)
                    nc.gpsimd.tensor_tensor(mixed[:, m, :], relu_k[:, m, :], relu_k[:, m, :], ALU.mult
                                            ).then_inc(squared, 1)
                if isinstance(c, int) and c == 0:
                    for t in range(TILES):
                        residual(0, t, 0, None)

            layernorm(0, None)
            clear_q(0, 1)
            run(pool, do_ab, do_c)

        @block.scalar
        def _(act):
            def do_ab(st, b, c, parity, finish=None):
                if b is None:
                    act.wait_ge(weights_split, len(weight))
                for n in range(NU):
                    if b is not None:
                        act.wait_ge(score_filled, NU * b + n + 1)
                        wait(act, lot_done, NL * b + (lot_of[n - NPB] + 1 if n >= NPB else lot_of[NU + n - NPB] + 1 - NL))
                        nc.scalar.activation(probs[:, n % NPB, :], score[n % NSB][:, :], ACT.Exp).then_inc(exp_done, 1)
                    if finish is not None and n in FINISH_HI_UNITS:
                        slot_of_c(finish, FINISH_HI_UNITS[n], b - 1, None, 1 - parity)
                    if b is not None and n >= GU and n % GU == COPY_AT:
                        copy_out(b, n // GU - 1)
                    if n == XT_AT - 1 + AHEAD and c is not None and exists(c + 1):
                        turn_x(st, c + 1)
                if c is not None:
                    bank_n, uses = st.slot("turned")
                    act.wait_ge(filled[bank_n], uses + 1)
                    wait(act, shift_in, 32 * c)
                    nc.scalar.mul(shifts[:, :], bank[bank_n][0:2 * PAIRS * TILES, 0:P], -1.0
                                  ).then_inc(drained[bank_n], 1)
                if b is not None:
                    copy_out(b, GROUPS - 1)

            def turn_x(st, c):
                wait(act, x_used, TILES * c)
                for m in range(CH):
                    bank_n, uses = st.slot(f"xT{m}")
                    act.wait_ge(filled[bank_n], uses + 1)
                    nc.scalar.copy(x_cols[:, m, 2:SEQ + 2], bank[bank_n][:, :]).then_inc(x_copied, 1)
                    nc.scalar.copy(xs[:, 0, m, :], bank[bank_n][:, :]).then_inc(drained[bank_n], 1)

            def scale_before(c, w, m):
                at = MIXES * c + CH * (1 - w) + m
                wait(act, mix_split, at + 1 - CH)
                wait(act, x_copied, CH * c + m + 1)
                nc.scalar.activation(mixed[:, m, :], x_cols[:, m, 1:SEQ + 1], ACT.Copy,
                                     scale=one_minus_mus[:, w, m:m + 1]).then_inc(mix_scaled, 1)

            def mix_hi_part(c, w, m):
                act.wait_ge(mix_summed, MIXES * c + CH * (1 - w) + m + 1)
                nc.scalar.copy((mix_k if w else xs)[:, 0, m, :], mixed[:, m, :]).then_inc(mix_hi, 1)

            def copy_out(b, g):
                act.wait_ge(lot_done, NL * b + 3 * (g + 1))
                nc.scalar.copy(o_cols[:, g, :], attn[:, :]).then_inc(o_copied, 1)

            def slot_of_c(st, name, b, c, parity):
                kind, m = name[:-1], int(name[-1])
                if kind in ("ot", "op", "wv"):
                    return
                if name == "r1":
                    act.wait_ge(q_stacked, QD * (c + 1))
                    for half in range(CH):
                        kf_bank, kf_uses = st.slot(f"kf{half}")
                        act.wait_ge(drained[kf_bank], kf_uses + 1)
                        nc.scalar.activation(split_a[:, 0, half, :], relu_k[:, half, :], ACT.Square).then_inc(act_hi, 1)
                bank_n, uses = st.slot(name)
                act.wait_ge(filled[bank_n], uses + 1)
                src = bank[bank_n][:, :]
                if kind == "q":
                    nc.scalar.mul(split_a[:, 0, m, :], src, SCALE).then_inc(qk_hi, 1)
                    scale_before(c, 1, m)
                if kind == "k":
                    nc.scalar.copy(split_b[:, 0, m, :], src).then_inc(qk_hi, 1)
                    mix_hi_part(c, 1, m)
                if kind == "v":
                    if isinstance(c, int) and c <= 1:
                        act.wait_ge(v_cleared[c], 1)
                    nc.scalar.copy(v_ones[parity][:, 2 * m:2 * m + 2, :, 0:DH],
                                   src.rearrange("p (t h d) -> p t h d", t=2, h=HEADS)
                                   ).then_inc(drained[bank_n], 1)
                    if m == 0:
                        scale_before(c, 0, 0)
                        scale_before(c, 0, 1)
                    else:
                        mix_hi_part(c, 0, 0)
                if kind == "kf":
                    wait(act, squared, CH * c)
                    nc.scalar.activation(relu_k[:, m, :], src, ACT.Relu).then_inc(drained[bank_n], 1)
                    if m == 0:
                        mix_hi_part(c, 0, 1)
                if kind == "oc":
                    nc.scalar.copy(mix_k[:, 0, m, :], src).then_inc(o_hi, 1)
                if kind == "r":
                    nc.scalar.activation(gate[:, m, :], src, ACT.Tanh, scale=0.5).then_inc(drained[bank_n], 1)

            def do_c(st, b, c, parity):
                for name in st.names:
                    slot_of_c(st, name, b, c, parity)

            for n, (name, w) in enumerate(weight.items()):
                act.wait_ge(weight_in[name], 16)
                nc.scalar.mul(w[:, 0, :, :], probs[:, n, :].rearrange("p (c d) -> p c d", c=CH),
                              0.5 if name == "fv" else 1.0).then_inc(weights_hi, 1)
            turn_x(Stage(0, 0, X_LIST), 0)
            act.wait_ge(mus_ready, 1)
            act.wait_ge(x_cols_cleared, 1)
            run(act, do_ab, do_c)

        @block.vector
        def _(dve):
            def ln_part(c, t):
                if t < TILES:
                    dve.wait_ge(x_loaded, 16 * (c + 1))
                    nc.vector.bn_stats(stats[:, t, :], x_in[:, t, :]).then_inc(bn_ready, 1)
                if t > 0:
                    dve.wait_ge(bn_ready, TILES * c + t)
                    alone(dve)
                    nc.vector.bn_aggr(mean_var[:, t - 1, :], stats[:, t - 1, :]).then_inc(moments_ready, 1)
                if t == TILES:
                    dve.wait_ge(moments_ready, TILES * (c + 1))
                    wait(dve, rows_ready, TILES * c)
                    nc.vector.tensor_scalar(neg_mean[:, :], mean_var[:, :, 0], -1.0, None, ALU.mult).then_inc(ln_scalars, 1)
                    nc.vector.tensor_scalar(var_eps[:, :], mean_var[:, :, 1], EPS, None, ALU.add).then_inc(ln_scalars, 1)

            def layernorm(c):
                for t in range(TILES + 1):
                    ln_part(c, t)

            def do_ab(st, b, c, parity, finish=None):
                if finish is not None:
                    do_c(finish, b - 1, None, 1 - parity)
                if b is None:
                    nc.vector.memset(attn[:, :], 0.0).then_inc(attn_cleared, 1)
                    dve.wait_ge(consts_ready, 7)
                if c is not None:
                    for n, (kind, pair, par) in enumerate(UNITS):
                        bank_n, uses = st.slot(n)
                        dve.wait_ge(filled[bank_n], uses + 1)
                        alone(dve)
                        for at, pr, tile in max_parts(kind, par):
                            keys = (tile + 1) * P
                            part = bank[bank_n][:, at:at + keys]
                            ins = nc.vector.tensor_tensor_reduce(
                                out=part, in0=part, in1=causal[:, SEQ - keys:SEQ], scale=1.0, scalar=LOWEST,
                                op0=ALU.add, op1=ALU.max, accum_out=maxes[:, pr, pair, tile:tile + 1])
                        ins.then_inc(drained[bank_n], 1)
                        if n in LN_UNITS and exists(c + 1):
                            ln_part(c + 1, LN_UNITS.index(n))

            def mix(c, w, m):
                dve.wait_ge(mix_scaled, MIXES * c + CH * (1 - w) + m + 1)
                nc.vector.scalar_tensor_tensor(mixed[:, m, :], x_cols[:, m, 2:SEQ + 2], mus[:, w, m:m + 1], mixed[:, m, :],
                                               ALU.mult, ALU.add).then_inc(mix_summed, 1)

            def mix_lo_part(c, w, m):
                dst = mix_k if w else xs
                dve.wait_ge(mix_hi, MIXES * c + CH * (1 - w) + m + 1)
                nc.vector.tensor_tensor(dst[:, 1, m, :], mixed[:, m, :], dst[:, 0, m, :].bitcast(f32), ALU.subtract
                                        ).then_inc(mix_split, 1)

            def do_c(st, b, c, parity):
                for name in st.names:
                    kind, m = name[:-1], int(name[-1])
                    bank_n, uses = st.slot(name)
                    src = bank[bank_n][:, :]
                    if kind == "q":
                        dve.wait_ge(qk_hi, 2 * CH * c + m + 1)
                        nc.vector.scalar_tensor_tensor(split_a[:, 1, m, :], src, SCALE, split_a[:, 0, m, :].bitcast(f32),
                                                       ALU.mult, ALU.subtract).then_inc(drained[bank_n], 1)
                        if m == 1:
                            mix(c, 1, 0)
                    if kind == "k":
                        dve.wait_ge(qk_hi, 2 * CH * c + CH + m + 1)
                        nc.vector.tensor_tensor(split_b[:, 1, m, :], src, split_b[:, 0, m, :].bitcast(f32),
                                                ALU.subtract).then_inc(drained[bank_n], 1)
                        if m == 0:
                            mix(c, 1, 1)
                        else:
                            mix_lo_part(c, 1, 0)
                    if name == "v0":
                        mix_lo_part(c, 1, 1)
                    if name == "v1":
                        mix(c, 0, 0)
                        mix(c, 0, 1)
                    if kind == "ot":
                        dve.wait_ge(filled[bank_n], uses + 1)
                        per_head = src.rearrange("p (h d) -> p h d", h=HEADS)
                        nc.vector.reciprocal(inv_den[:, m, :], per_head[:, :, DH]).then_inc(inv_ready, 1)
                        dve.wait_ge(inv_ready, TILES * b + m + 1)
                        nc.vector.tensor_tensor(rows[:, m, :].rearrange("p (h d) -> p h d", h=HEADS), per_head[:, :, 0:DH],
                                                inv_den[:, m, :].unsqueeze(2).to_broadcast([P, HEADS, DH]), ALU.mult
                                                ).then_inc(drained[bank_n], 1)
                    if kind == "kf":
                        mix_lo_part(c, 0, m)
                    if name == "r1":
                        for half in range(CH):
                            dve.wait_ge(act_hi, CH * c + half + 1)
                            dve.wait_ge(squared, CH * c + half + 1)
                            nc.vector.tensor_tensor(split_a[:, 1, half, :], mixed[:, half, :],
                                                    split_a[:, 0, half, :].bitcast(f32), ALU.subtract).then_inc(act_split, 1)
                    if kind == "oc":
                        dve.wait_ge(o_hi, CH * b + m + 1)
                        nc.vector.tensor_tensor(mix_k[:, 1, m, :], src, mix_k[:, 0, m, :].bitcast(f32),
                                                ALU.subtract).then_inc(drained[bank_n], 1)
                    if kind == "op":
                        dve.wait_ge(filled[bank_n], uses + 1)
                        dve.wait_ge(x_used, TILES * (b + 1))
                        nc.vector.tensor_tensor(acc[parity][:, 2 * m:2 * m + 2, :], src.rearrange("p (t d) -> p t d", t=2),
                                                acc[parity][:, 2 * m:2 * m + 2, :], ALU.add).then_inc(drained[bank_n], 1)
                    if kind == "wv":
                        dve.wait_ge(filled[bank_n], uses + 1)
                        r_bank, r_uses = st.slot(f"r{m}")
                        dve.wait_ge(drained[r_bank], r_uses + 1)
                        nc.vector.scalar_tensor_tensor(gate[:, m, :], gate[:, m, :], 1.0, src, ALU.add, ALU.mult
                                                       ).then_inc(drained[bank_n], 1)

            nc.vector.memset(x_cols[:, :, 0:2], 0.0).then_inc(x_cols_cleared, 1)
            nc.vector.memset(q_stack[0][:, 0, :, :].bitcast(f32), 0.0).then_inc(q_cleared[0], 1)
            layernorm(0)
            nc.vector.memset(k_stack[0][:, :, :].bitcast(f32), 0.0).then_inc(k_cleared[0], 1)
            nc.vector.memset(v_ones[0][:, :, :, :], 1.0).then_inc(v_cleared[0], 1)
            for n, (name, w) in enumerate(weight.items()):
                if n == 2:
                    for m in range(CH):
                        bank_n, uses = Stage(0, 0, X_LIST).slot(f"xT{m}")
                        dve.wait_ge(drained[bank_n], uses + 1)
                        nc.vector.tensor_tensor(xs[:, 1, m, :], x_cols[:, m, 2:SEQ + 2], xs[:, 0, m, :].bitcast(f32),
                                                ALU.subtract).then_inc(x_split, 1)
                dve.wait_ge(weights_hi, n + 1)
                nc.vector.scalar_tensor_tensor(w[:, 1, :, :], probs[:, n, :].rearrange("p (c d) -> p c d", c=CH),
                                               0.5 if name == "fv" else 1.0, w[:, 0, :, :].bitcast(f32),
                                               ALU.mult, ALU.subtract).then_inc(weights_split, 1)
            dve.wait_ge(mus_in, 16)
            nc.vector.tensor_scalar(one_minus_mus[:, :, :], mus[:, :, :], -1.0, 1.0, ALU.mult, ALU.add
                                    ).then_inc(mus_ready, 1)
            run(dve, do_ab, do_c)

        @block.tensor
        def _(pe):
            pe.wait_ge(consts_ready, 6)

            def open_slot(st, name):
                bank_n, uses = st.slot(name)
                wait(pe, drained[bank_n], uses)
                return bank_n, bank[bank_n]

            def maxima(st, c, n, parity):
                kind, pair, par = UNITS[n]
                qs, ks = q_stack[parity], k_stack[parity]
                bank_n, dst = open_slot(st, n)
                for at, pr, tile in max_parts(kind, par):
                    keys = (tile + 1) * P
                    ins = nc.tensor.matmul(dst[:, at:at + keys], qs[:, pr, pair, tile * P:(tile + 1) * P],
                                           ks[:, pair, 0:keys], start=True, stop=True)
                ins.then_inc(filled[bank_n], 1)

            def scores(b, n, parity):
                kind, pair, par = UNITS[n]
                qs, ks = q_stack[parity], k_stack[parity]
                dst = score[n % NSB]
                before = n - NSB if n >= NSB else NU - 1 - (NU - 1 - n) % NSB - NU
                wait(pe, exp_done, NU * b + before + 1)
                if kind == 0:
                    parts = [(0, par, 0)]
                if kind == 1:
                    parts = [(0, par, 1), (SEQ - P, par, 3)]
                if kind == 2:
                    parts = [(0, 0, 2), (SEQ // 2, 1, 2)]
                for at, pr, tile in parts:
                    queries = SEQ - tile * P
                    ins = nc.tensor.matmul(dst[:, at:at + queries], ks[:, pair, tile * P:(tile + 1) * P],
                                           qs[:, pr, pair, tile * P:SEQ], start=True, stop=True)
                ins.then_inc(score_filled, 1)

            def lot(b, n, parity):
                first, end = LOTS[n]
                g = n // 3
                if n % 3 == 0:
                    wait(pe, o_copied, GROUPS * b + g)
                pe.wait_ge(masked, NU * b + end)
                todo = []
                for u in range(first, end):
                    kind, pair, par = UNITS[u]
                    if kind == 0:
                        todo += [(0, u, pair, par, 0, 0)]
                    if kind == 1:
                        todo += [(0, u, pair, par, 0, 1), (1, u, pair, par, SEQ - P, 3)]
                    if kind == 2:
                        todo += [(0, u, pair, 0, 0, 2), (0, u, pair, 1, SEQ // 2, 2)]
                todo.sort(key=lambda x: x[0])
                for _, u, pair, par, at, tile in todo:
                    quad = (pair % 2) * 2 + par
                    head = 4 * g + quad
                    queries = SEQ - tile * P
                    ins = nc.tensor.matmul(attn[32 * quad:32 * quad + VW, tile * P:SEQ],
                                           v_ones[parity][:, tile, head, :], probs[:, u % NPB, at:at + queries],
                                           start=(tile == 0), stop=(tile == 2), skip_group_check=True)
                ins.then_inc(lot_done, 1)

            def do_ab(st, b, c, parity, finish=None):
                if c is not None:
                    pe.wait_ge(q_stacked, QD * (c + 1))
                    pe.wait_ge(k_stacked, KD * (c + 1))
                    pe.wait_ge(shift_zeroed, 32 * (c + 1))
                    if isinstance(c, int) and c <= 1:
                        pe.wait_ge(ones_in[c], 32)
                if b is None:
                    pe.wait_ge(attn_cleared, 1)
                    pe.wait_ge(weights_split, len(weight))
                if b is not None:
                    pe.wait_ge(shift_in, 32 * (b + 1))
                todo = list(range(NL))
                for n in range(-AHEAD, NU):
                    if n == XT_AT and c is not None and exists(c + 1):
                        turn_x(st, c + 1)
                    if c is not None and n >= 0:
                        maxima(st, c, n, 1 - parity)
                    ahead = n + AHEAD
                    if b is not None and ahead < NU:
                        scores(b, ahead, parity)
                    if finish is not None and ahead in FINISH_UNITS:
                        slot_of_c(finish, FINISH_UNITS[ahead], b - 1, None, 1 - parity)
                    if b is not None and todo and LOTS[todo[0]][1] - 1 + LAG <= ahead:
                        lot(b, todo.pop(0), parity)
                if c is not None:
                    bank_n, dst = open_slot(st, "turned")
                    last, uses = st.slot(NU - 1)
                    pe.wait_ge(drained[last], uses + 1)
                    alone(pe)
                    nc.tensor.transpose(dst[0:2 * PAIRS * TILES, 0:P], maxes[:, :, :, :].rearrange("p a b c -> p (a b c)"),
                                        ident[:, :]).then_inc(filled[bank_n], 1)
                if b is not None:
                    for n in todo:
                        lot(b, n, parity)

            def turn_x(st, c):
                for m in range(CH):
                    bank_n, dst = open_slot(st, f"xT{m}")
                    pe.wait_ge(rows_ready, TILES * (c + 1))
                    alone(pe)
                    for t in range(TILES):
                        ins = nc.tensor.transpose(dst[:, t * P:(t + 1) * P], rows[:, t, m * P:(m + 1) * P], ident[:, :])
                    ins.then_inc(filled[bank_n], 1)

            def products(dst, pairs):
                for n, (lhs, rhs) in enumerate(pairs):
                    ins = nc.tensor.matmul(dst, lhs, rhs, start=(n == 0), stop=(n == len(pairs) - 1))
                return ins

            SPLIT = ((0, 0), (0, 1), (1, 0))

            def columns(dst, m, a, w):
                return products(dst[:, :], [(w[:, pw, c, m * P:(m + 1) * P], a(pa, c)) for pa, pw in SPLIT for c in range(CH)])

            def tokens(dst, m, a, w):
                for i in range(2):
                    cut = slice((2 * m + i) * P, (2 * m + i + 1) * P)
                    ins = products(dst[:, i * D:(i + 1) * D],
                                   [(a(pa, c)[:, cut], w[:, pw, c, :]) for pa, pw in SPLIT for c in range(CH)])
                return ins

            def part_x(part, c):
                return xs[:, part, c, :]

            def part_k(part, c):
                return mix_k[:, part, c, :]

            def part_a(part, c):
                return split_a[:, part, c, :]

            def slot_of_c(st, name, b, c, parity):
                kind, m = name[:-1], int(name[-1])
                bank_n, dst = open_slot(st, name)
                if isinstance(c, int) and c == 0 and kind in ("q", "k", "v", "kf", "r", "wv"):
                    name_of = {"kf": "fk", "r": "fr", "wv": "fv"}.get(kind, kind)
                    pe.wait_ge(weights_split, list(weight).index(name_of) + 1)
                if kind in ("q", "k"):
                    if name == "q0":
                        pe.wait_ge(x_split, CH * (c + 1))
                    ins = columns(dst, m, part_x, weight[kind])
                if kind == "v":
                    ins = tokens(dst, m, part_x, weight["v"])
                if kind == "kf":
                    pe.wait_ge(mix_split, MIXES * c + CH)
                    ins = columns(dst, m, part_k, weight["fk"])
                if kind == "r":
                    pe.wait_ge(mix_split, MIXES * (c + 1))
                    ins = tokens(dst, m, part_x, weight["fr"])
                if kind == "ot":
                    wait(pe, o_copied, GROUPS * (b + 1))
                    for g in range(GROUPS):
                        ins = nc.tensor.transpose(dst[:, g * P:(g + 1) * P], o_cols[:, g, m * P:(m + 1) * P], ident[:, :])
                if kind == "oc":
                    for t in range(TILES):
                        if m == 0:
                            t_bank, uses = st.slot(f"ot{t}")
                            pe.wait_ge(drained[t_bank], uses + 1)
                        ins = nc.tensor.transpose(dst[:, t * P:(t + 1) * P], rows[:, t, m * P:(m + 1) * P], ident[:, :])
                if kind == "op":
                    if m == 0:
                        for o_name in ("oc0", "oc1"):
                            o_bank, uses = st.slot(o_name)
                            pe.wait_ge(drained[o_bank], uses + 1)
                    ins = tokens(dst, m, part_k, weight["o"])
                if kind == "wv":
                    pe.wait_ge(act_split, CH * (c + 1))
                    ins = tokens(dst, m, part_a, weight["fv"])
                ins.then_inc(filled[bank_n], 1)

            def do_c(st, b, c, parity):
                for name in st.names:
                    slot_of_c(st, name, b, c, parity)

            turn_x(Stage(0, 0, X_LIST), 0)
            run(pe, do_ab, do_c)


def kernel(L0_attn_X, L0_attn_q_proj, L0_attn_k_proj, L0_attn_v_proj, L0_attn_o_proj,
           L0_ffn_W_r, L0_ffn_W_k, L0_ffn_W_v, L0_ffn_mu_r, L0_ffn_mu_k):
    import numpy as np
    import concourse.bacc as bacc
    from concourse.bass_utils import run_bass_kernel_spmd

    D, DH, P = 256, 16, 128

    def chunks(w):
        return np.ascontiguousarray(w.reshape(D // P, P, D).transpose(1, 0, 2).reshape(P, -1))

    def arr(a):
        return np.asarray(a)

    def for_stack(w):
        return arr(w).reshape(2, 4, 2, DH, D).transpose(4, 0, 2, 3, 1).reshape(D, D)

    data = {
        "x": arr(L0_attn_X),
        "wq_t": chunks(for_stack(L0_attn_q_proj)),
        "wk_t": chunks(for_stack(L0_attn_k_proj)),
        "wv_t": chunks(arr(L0_attn_v_proj).reshape(2, 4, 2, DH, D).transpose(4, 1, 0, 2, 3).reshape(D, D)),
        "wo_t": chunks(arr(L0_attn_o_proj).reshape(D, 2, 4, 2, DH).transpose(2, 1, 3, 4, 0).reshape(D, D)),
        "fr_t": chunks(arr(L0_ffn_W_r).T),
        "fk_t": chunks(arr(L0_ffn_W_k).T),
        "fv_t": chunks(arr(L0_ffn_W_v).T),
        "mu": np.ascontiguousarray(np.stack([arr(L0_ffn_mu_r), arr(L0_ffn_mu_k)]).reshape(2, D // P, P).transpose(2, 0, 1)),
    }
    nc = bacc.Bacc("TRN2", target_bir_lowering=False, num_devices=1, dynamic_dma_scratch_size=1024)
    args = {n: nc.dram_tensor(n, a.shape, mybir.dt.from_np(a.dtype), kind="ExternalInput").ap() for n, a in data.items()}
    out = nc.dram_tensor("out", data["x"].shape, mybir.dt.float32, kind="ExternalOutput").ap()
    attention_and_channel_mix(nc, **args, out=out)
    got = run_bass_kernel_spmd(nc, [data], core_ids=[0])
    return got.results[0]["out"]
```
